# Optimizing a Trainium2 kernel written in Bass

```python
import numpy as np
import jax
import jax.numpy as jnp

def _softmax(x, axis=-1):
    return jax.nn.softmax(x, axis=axis)

def _gelu(x):
    return jax.nn.gelu(x, approximate=True)

def _silu(x):
    return jax.nn.silu(x)

def _sigmoid(x):
    return jax.nn.sigmoid(x)

def _layernorm(x, axis=-1, eps=1e-05):
    m = jnp.mean(x, axis=axis, keepdims=True)
    v = jnp.var(x, axis=axis, keepdims=True)
    return (x - m) / jnp.sqrt(v + eps)

def _scatter_add(tgt, idx, src, axis=0):
    return tgt.at[idx].add(src)

def _segment_sum(src, seg, n):
    return jax.ops.segment_sum(src, seg, n)
kernel_name = 'mk_gnn_ffn_d4_gnn_r32_9fc779'

def setup_inputs(seed: int=0):
    np.random.seed(seed)
    _w = jnp.asarray

    def _rec_inputs():
        import jax
        import jax.numpy as jnp
        _gk = jax.random.key(seed)
        x = -0.0002117 + 1 * jax.random.normal(jax.random.fold_in(_gk, 1), (3125, 256), jnp.float32)
        src = jax.random.randint(jax.random.fold_in(_gk, 2), (50000,), 0, 3125, jnp.int32)
        dst = jnp.minimum((3125 * jax.random.uniform(jax.random.fold_in(_gk, 3), (50000,)) ** 2.0).astype(jnp.int32), 99999)
        _o = jnp.argsort(dst, stable=True)
        src = src[_o]
        dst = dst[_o]
        return (x, src, dst)
    x, src, dst = _rec_inputs()

    def _L0_gnn_setup():
        import jax, jax.numpy as jnp
        import numpy as np
        N = 3125
        E = 50000
        IN = 256
        OUT = 64
        H = 4
        SLOPE = 0.01
        key = jax.random.key(seed)
        k1, k2, k3, k4, k5 = jax.random.split(key, 5)
        h = jax.random.normal(k1, (N, IN), dtype=jnp.float32)
        W = jax.random.normal(k2, (H, OUT, IN), dtype=jnp.float32) * (1.0 / np.sqrt(IN))
        attn = jax.random.normal(k3, (H, 2 * OUT), dtype=jnp.float32) * (1.0 / np.sqrt(2 * OUT))
        edge_src = jax.random.randint(k4, (E,), 0, N, dtype=jnp.int32)
        edge_dst = jax.random.randint(k5, (E,), 0, N, dtype=jnp.int32)
        return {'h': h, 'W': W, 'attn': attn, 'edge_src': edge_src, 'edge_dst': edge_dst}
    _L0_gnn_all = _L0_gnn_setup()
    _L0_gnn_in = {k: v for k, v in _L0_gnn_all.items() if k in ('W', 'attn')}
    del _L0_gnn_all

    def _L0_ffn_setup():
        import math
        import jax, jax.numpy as jnp
        import numpy as np
        CAPACITY_FACTOR = 1.25
        key = jax.random.key(seed)
        ks = jax.random.split(key, 5)
        B, L, D, F, E = (8, 256, 256, 1024, 8)
        h = jax.random.normal(ks[0], (B, L, D), dtype=jnp.float32)
        gate_w = jax.random.normal(ks[1], (D, E), dtype=jnp.float32) * 0.02
        gate_b = jnp.zeros((E,), dtype=jnp.float32)
        w1 = jax.random.normal(ks[2], (E, D, F), dtype=jnp.float32) * (1.0 / math.sqrt(D))
        b1 = jnp.zeros((E, F), dtype=jnp.float32)
        w2 = jax.random.normal(ks[3], (E, F, D), dtype=jnp.float32) * (1.0 / math.sqrt(F))
        b2 = jnp.zeros((E, D), dtype=jnp.float32)
        return {'h': h, 'gate_w': gate_w, 'gate_b': gate_b, 'w1': w1, 'b1': b1, 'w2': w2, 'b2': b2}
    _L0_ffn_all = _L0_ffn_setup()
    _L0_ffn_in = {k: v for k, v in _L0_ffn_all.items() if k in ('gate_w', 'gate_b', 'w1', 'b1', 'w2', 'b2')}
    del _L0_ffn_all

    def _L1_gnn_setup():
        import jax, jax.numpy as jnp
        import numpy as np
        N = 10000
        E = 10000
        D = 256
        key = jax.random.key(seed)
        ks = jax.random.split(key, 10)
        s = 1.0 / np.sqrt(D)
        return {'x0': jax.random.normal(ks[0], (N, D), jnp.float32), 'edge_index': jax.random.randint(ks[1], (2, E), 0, N, jnp.int32), 'W1': jax.random.normal(ks[2], (D, D), jnp.float32) * s, 'b1': jax.random.normal(ks[3], (D,), jnp.float32) * s, 'W2': jax.random.normal(ks[4], (D, D), jnp.float32) * s, 'b2': jax.random.normal(ks[5], (D,), jnp.float32) * s, 'wa1': jax.random.normal(ks[6], (D,), jnp.float32) * s, 'ba1': jax.random.normal(ks[7], (1,), jnp.float32) * s, 'wa2': jax.random.normal(ks[8], (D,), jnp.float32) * s, 'ba2': jax.random.normal(ks[9], (1,), jnp.float32) * s}
    _L1_gnn_all = _L1_gnn_setup()
    _L1_gnn_in = {k: v for k, v in _L1_gnn_all.items() if k in ('W1', 'b1', 'W2', 'b2', 'wa1', 'ba1', 'wa2', 'ba2')}
    del _L1_gnn_all

    def _L1_ffn_setup():
        import jax, jax.numpy as jnp
        import numpy as np
        B, S, D, H, E, K = (8, 256, 256, 1024, 8, 2)
        key = jax.random.key(seed)
        ks = jax.random.split(key, 7)
        s_in = 1.0 / np.sqrt(D)
        s_hid = 1.0 / np.sqrt(H)
        return {'x': jax.random.normal(ks[0], (B, S, D), dtype=jnp.float32), 'Wg': jax.random.uniform(ks[1], (E, D), jnp.float32, -s_in, s_in), 'bg': jax.random.uniform(ks[2], (E,), jnp.float32, -s_in, s_in), 'W1': jax.random.uniform(ks[3], (E, H, D), jnp.float32, -s_in, s_in), 'b1': jax.random.uniform(ks[4], (E, H), jnp.float32, -s_in, s_in), 'W2': jax.random.uniform(ks[5], (E, D, H), jnp.float32, -s_hid, s_hid), 'b2': jax.random.uniform(ks[6], (E, D), jnp.float32, -s_hid, s_hid)}
    _L1_ffn_all = _L1_ffn_setup()
    _L1_ffn_in = {k: v for k, v in _L1_ffn_all.items() if k in ('Wg', 'bg', 'W1', 'b1', 'W2', 'b2')}
    del _L1_ffn_all

    def _L2_gnn_setup():
        import jax, jax.numpy as jnp
        import numpy as np
        N_NODES = 3125
        N_EDGES = 50000
        IN_FEATS = 256
        OUT_FEATS = 256
        key = jax.random.key(seed)
        k1, k2, k3, k4, k5, k6 = jax.random.split(key, 6)
        h = jax.random.normal(k1, (N_NODES, IN_FEATS), dtype=jnp.float32)
        norm = jax.random.uniform(k2, (N_NODES, 1), dtype=jnp.float32)
        W = jax.random.normal(k3, (OUT_FEATS, IN_FEATS), dtype=jnp.float32) * (1.0 / np.sqrt(IN_FEATS))
        b = jax.random.normal(k4, (OUT_FEATS,), dtype=jnp.float32) * 0.01
        src = jax.random.randint(k5, (N_EDGES,), 0, N_NODES, dtype=jnp.int32)
        dst = jax.random.randint(k6, (N_EDGES,), 0, N_NODES, dtype=jnp.int32)
        return {'h': h, 'norm': norm, 'W': W, 'b': b, 'src': src, 'dst': dst}
    _L2_gnn_all = _L2_gnn_setup()
    _L2_gnn_in = {k: v for k, v in _L2_gnn_all.items() if k in ('W', 'b')}
    del _L2_gnn_all

    def _L2_ffn_setup():
        import jax, jax.numpy as jnp
        import numpy as np
        E = 8
        K = 2
        D = 256
        H = 512
        DOUT = 256
        EPS = 1e-05
        key = jax.random.key(seed)
        ks = jax.random.split(key, 9)
        s = 0.02
        return {'x': jax.random.normal(ks[0], (4, 256, D), jnp.float32), 'gamma': 1.0 + 0.05 * jax.random.normal(ks[1], (D,), jnp.float32), 'beta': 0.05 * jax.random.normal(ks[2], (D,), jnp.float32), 'Wr': 0.01 * jax.random.normal(ks[3], (D, E), jnp.float32), 'br': jnp.zeros((E,), jnp.float32), 'W1': s * jax.random.normal(ks[4], (E, D, H), jnp.float32), 'b1': s * jax.random.normal(ks[5], (E, H), jnp.float32), 'W2': s * jax.random.normal(ks[6], (E, H, DOUT), jnp.float32), 'b2': s * jax.random.normal(ks[7], (E, DOUT), jnp.float32)}
    _L2_ffn_all = _L2_ffn_setup()
    _L2_ffn_in = {k: v for k, v in _L2_ffn_all.items() if k in ('gamma', 'beta', 'Wr', 'br', 'W1', 'b1', 'W2', 'b2')}
    del _L2_ffn_all

    def _L3_gnn_setup():
        import jax, jax.numpy as jnp
        import numpy as np
        N_NODES = 50000
        N_EDGES = 25000
        D_IN = 256
        D_OUT = 256
        BN_EPS = 1e-05

        def _forward(x, edge_index, w1, b1, gamma, beta, w2, b2, w_gcn, b_gcn):
            n = x.shape[0]
            h = x @ w1.T + b1
            mean = jnp.mean(h, axis=0)
            var = jnp.var(h, axis=0)
            h = (h - mean) * jax.lax.rsqrt(var + BN_EPS) * gamma + beta
            h = jax.nn.relu(h)
            h = h @ w2.T + b2
            xw = h @ w_gcn.T
            src = jnp.concatenate([edge_index[0], jnp.arange(n, dtype=edge_index.dtype)])
            dst = jnp.concatenate([edge_index[1], jnp.arange(n, dtype=edge_index.dtype)])
            deg = jax.ops.segment_sum(jnp.ones_like(dst, dtype=xw.dtype), dst, num_segments=n)
            dinv = jnp.where(deg > 0, jax.lax.rsqrt(jnp.maximum(deg, 1.0)), 0.0)
            norm = dinv[src] * dinv[dst]
            msgs = xw[src] * norm[:, None]
            out = jax.ops.segment_sum(msgs, dst, num_segments=n) + b_gcn
            return out
        key = jax.random.key(seed)
        ks = jax.random.split(key, 8)
        x = jax.random.normal(ks[0], (N_NODES, D_IN), dtype=jnp.float32)
        edge_index = jax.random.randint(ks[1], (2, N_EDGES), 0, N_NODES, dtype=jnp.int64)
        s1 = 1.0 / np.sqrt(D_IN)
        s2 = 1.0 / np.sqrt(D_OUT)
        w1 = jax.random.uniform(ks[2], (D_OUT, D_IN), jnp.float32, -s1, s1)
        b1 = jax.random.uniform(ks[3], (D_OUT,), jnp.float32, -s1, s1)
        gamma = jnp.ones((D_OUT,), jnp.float32)
        beta = jnp.zeros((D_OUT,), jnp.float32)
        w2 = jax.random.uniform(ks[4], (D_OUT, D_OUT), jnp.float32, -s2, s2)
        b2 = jax.random.uniform(ks[5], (D_OUT,), jnp.float32, -s2, s2)
        w_gcn = jax.random.uniform(ks[6], (D_OUT, D_OUT), jnp.float32, -s2, s2)
        b_gcn = jnp.zeros((D_OUT,), jnp.float32)
        return {'x': x, 'edge_index': edge_index, 'w1': w1, 'b1': b1, 'gamma': gamma, 'beta': beta, 'w2': w2, 'b2': b2, 'w_gcn': w_gcn, 'b_gcn': b_gcn}
    _L3_gnn_all = _L3_gnn_setup()
    _L3_gnn_in = {k: v for k, v in _L3_gnn_all.items() if k in ('w1', 'b1', 'gamma', 'beta', 'w2', 'b2', 'w_gcn', 'b_gcn')}
    del _L3_gnn_all

    def _L3_ffn_setup():
        import jax, jax.numpy as jnp
        import numpy as np
        B, S, D, E, H, K = (4, 128, 256, 8, 512, 2)
        key = jax.random.key(seed)
        ks = jax.random.split(key, 6)
        x = jax.random.normal(ks[0], (B, S, D), jnp.float32)
        Wg = jax.random.normal(ks[1], (D, E), jnp.float32) * 0.02
        bg = jnp.zeros((E,), jnp.float32)
        W1 = jax.random.normal(ks[2], (E, D, H), jnp.float32) * 0.02
        b1 = jnp.zeros((E, H), jnp.float32)
        W2 = jax.random.normal(ks[3], (E, H, D), jnp.float32) * 0.02
        b2 = jnp.zeros((E, D), jnp.float32)
        return {'x': x, 'Wg': Wg, 'bg': bg, 'W1': W1, 'b1': b1, 'W2': W2, 'b2': b2}
    _L3_ffn_all = _L3_ffn_setup()
    _L3_ffn_in = {k: v for k, v in _L3_ffn_all.items() if k in ('Wg', 'bg', 'W1', 'b1', 'W2', 'b2')}
    del _L3_ffn_all
    return {'x': x, 'src': src, 'dst': dst, 'L0_gnn_W': _L0_gnn_in['W'], 'L0_gnn_attn': _L0_gnn_in['attn'], 'L0_ffn_gate_w': _L0_ffn_in['gate_w'], 'L0_ffn_gate_b': _L0_ffn_in['gate_b'], 'L0_ffn_w1': _L0_ffn_in['w1'], 'L0_ffn_b1': _L0_ffn_in['b1'], 'L0_ffn_w2': _L0_ffn_in['w2'], 'L0_ffn_b2': _L0_ffn_in['b2'], 'L1_gnn_W1': _L1_gnn_in['W1'], 'L1_gnn_b1': _L1_gnn_in['b1'], 'L1_gnn_W2': _L1_gnn_in['W2'], 'L1_gnn_b2': _L1_gnn_in['b2'], 'L1_gnn_wa1': _L1_gnn_in['wa1'], 'L1_gnn_ba1': _L1_gnn_in['ba1'], 'L1_gnn_wa2': _L1_gnn_in['wa2'], 'L1_gnn_ba2': _L1_gnn_in['ba2'], 'L1_ffn_Wg': _L1_ffn_in['Wg'], 'L1_ffn_bg': _L1_ffn_in['bg'], 'L1_ffn_W1': _L1_ffn_in['W1'], 'L1_ffn_b1': _L1_ffn_in['b1'], 'L1_ffn_W2': _L1_ffn_in['W2'], 'L1_ffn_b2': _L1_ffn_in['b2'], 'L2_gnn_W': _L2_gnn_in['W'], 'L2_gnn_b': _L2_gnn_in['b'], 'L2_ffn_gamma': _L2_ffn_in['gamma'], 'L2_ffn_beta': _L2_ffn_in['beta'], 'L2_ffn_Wr': _L2_ffn_in['Wr'], 'L2_ffn_br': _L2_ffn_in['br'], 'L2_ffn_W1': _L2_ffn_in['W1'], 'L2_ffn_b1': _L2_ffn_in['b1'], 'L2_ffn_W2': _L2_ffn_in['W2'], 'L2_ffn_b2': _L2_ffn_in['b2'], 'L3_gnn_w1': _L3_gnn_in['w1'], 'L3_gnn_b1': _L3_gnn_in['b1'], 'L3_gnn_gamma': _L3_gnn_in['gamma'], 'L3_gnn_beta': _L3_gnn_in['beta'], 'L3_gnn_w2': _L3_gnn_in['w2'], 'L3_gnn_b2': _L3_gnn_in['b2'], 'L3_gnn_w_gcn': _L3_gnn_in['w_gcn'], 'L3_gnn_b_gcn': _L3_gnn_in['b_gcn'], 'L3_ffn_Wg': _L3_ffn_in['Wg'], 'L3_ffn_bg': _L3_ffn_in['bg'], 'L3_ffn_W1': _L3_ffn_in['W1'], 'L3_ffn_b1': _L3_ffn_in['b1'], 'L3_ffn_W2': _L3_ffn_in['W2'], 'L3_ffn_b2': _L3_ffn_in['b2']}

def reference(x, src, dst, L0_gnn_W, L0_gnn_attn, L0_ffn_gate_w, L0_ffn_gate_b, L0_ffn_w1, L0_ffn_b1, L0_ffn_w2, L0_ffn_b2, L1_gnn_W1, L1_gnn_b1, L1_gnn_W2, L1_gnn_b2, L1_gnn_wa1, L1_gnn_ba1, L1_gnn_wa2, L1_gnn_ba2, L1_ffn_Wg, L1_ffn_bg, L1_ffn_W1, L1_ffn_b1, L1_ffn_W2, L1_ffn_b2, L2_gnn_W, L2_gnn_b, L2_ffn_gamma, L2_ffn_beta, L2_ffn_Wr, L2_ffn_br, L2_ffn_W1, L2_ffn_b1, L2_ffn_W2, L2_ffn_b2, L3_gnn_w1, L3_gnn_b1, L3_gnn_gamma, L3_gnn_beta, L3_gnn_w2, L3_gnn_b2, L3_gnn_w_gcn, L3_gnn_b_gcn, L3_ffn_Wg, L3_ffn_bg, L3_ffn_W1, L3_ffn_b1, L3_ffn_W2, L3_ffn_b2):
    import jax
    import jax.numpy as jnp

    def _L0_gnn_ref(h, W, attn, edge_src, edge_dst):
        import jax, jax.numpy as jnp
        import numpy as np
        N = 3125
        E = 50000
        IN = 256
        OUT = 64
        H = 4
        SLOPE = 0.01
        a0 = attn[0]
        a_src, a_dst = (a0[:OUT], a0[OUT:])
        outs = []
        for hd in range(H):
            z = h @ W[hd].T
            s_src = z @ a_src
            s_dst = z @ a_dst
            e = jax.nn.leaky_relu(s_src[edge_src] + s_dst[edge_dst], SLOPE)
            m = jax.ops.segment_max(e, edge_dst, num_segments=N)
            m = jnp.where(jnp.isfinite(m), m, 0.0)
            ex = jnp.exp(e - m[edge_dst])
            den = jax.ops.segment_sum(ex, edge_dst, num_segments=N)
            alpha = ex / jnp.maximum(den[edge_dst], 1e-09)
            msg = alpha[:, None] * z[edge_src]
            outs.append(jax.ops.segment_sum(msg, edge_dst, num_segments=N))
        return jnp.concatenate(outs, axis=1)

    def _L0_ffn_ref(h, gate_w, gate_b, w1, b1, w2, b2):
        import math
        import jax, jax.numpy as jnp
        import numpy as np
        CAPACITY_FACTOR = 1.25
        B, L, D = h.shape
        E = gate_w.shape[1]
        T = B * L
        C = max(1, math.ceil(CAPACITY_FACTOR * T / E))
        x = h.reshape(T, D)
        logits = x @ gate_w + gate_b
        probs = jax.nn.softmax(logits, axis=-1)
        idx = jnp.argmax(probs, axis=-1)
        prb = jnp.take_along_axis(probs, idx[:, None], axis=1)[:, 0]
        one_hot = jax.nn.one_hot(idx, E, dtype=jnp.float32)
        pos = (jnp.cumsum(one_hot, axis=0) * one_hot).sum(-1).astype(jnp.int32) - 1
        kept = pos < C
        pos_safe = jnp.where(kept, pos, C)
        buf = jnp.zeros((E, C, D), dtype=h.dtype).at[idx, pos_safe].set(x, mode='drop')
        hmid = jax.nn.relu(jnp.einsum('ecd,edf->ecf', buf, w1) + b1[:, None, :])
        ybuf = jnp.einsum('ecf,efd->ecd', hmid, w2) + b2[:, None, :]
        pos_g = jnp.minimum(pos, C - 1)
        y_tok = ybuf[idx, pos_g] * (prb * kept)[:, None]
        y = y_tok.reshape(B, L, D)
        y = jnp.nan_to_num(y, nan=0.0, posinf=10000.0, neginf=-10000.0)
        return y

    def _L1_gnn_ref(x0, edge_index, W1, b1, W2, b2, wa1, ba1, wa2, ba2):
        import jax, jax.numpy as jnp
        import numpy as np
        N = 10000
        E = 10000
        D = 256
        n = x0.shape[0]
        leaky = lambda v: jax.nn.leaky_relu(v, 0.2)
        x0_i = leaky(x0 @ W1 + b1)
        x0_j = leaky(x0 @ W2 + b2)
        a1 = x0_i @ wa1 + ba1[0]
        a2 = x0_j @ wa2 + ba2[0]
        row, col = (edge_index[0], edge_index[1])
        att = jax.nn.sigmoid(a1[row] + a2[col])
        msg = att[:, None] * x0_j[col]
        out = jax.ops.segment_sum(msg, row, num_segments=n)
        return out + x0

    def _L1_ffn_ref(x, Wg, bg, W1, b1, W2, b2):
        import jax, jax.numpy as jnp
        import numpy as np
        B, S, D, H, E, K = (8, 256, 256, 1024, 8, 2)
        gate_scores = jnp.einsum('bsd,ed->bse', x, Wg) + bg
        topk_scores, topk_idx = jax.lax.top_k(gate_scores, K)
        topk_probs = jax.nn.softmax(topk_scores, axis=-1)
        combine = jnp.sum(topk_probs[..., None] * jax.nn.one_hot(topk_idx, E, dtype=x.dtype), axis=-2)
        out = jnp.zeros_like(x)
        for e in range(E):
            h = jax.nn.relu(jnp.einsum('bsd,hd->bsh', x, W1[e]) + b1[e])
            y = jnp.einsum('bsh,dh->bsd', h, W2[e]) + b2[e]
            out = out + combine[..., e:e + 1] * y
        return out

    def _L2_gnn_ref(h, norm, W, b, src, dst):
        import jax, jax.numpy as jnp
        import numpy as np
        N_NODES = 3125
        N_EDGES = 50000
        IN_FEATS = 256
        OUT_FEATS = 256
        x = h @ W.T + b
        x = norm * x
        msg = x[src]
        agg = jax.ops.segment_sum(msg, dst, num_segments=h.shape[0])
        return agg * norm

    def _L2_ffn_ref(x, gamma, beta, Wr, br, W1, b1, W2, b2):
        import jax, jax.numpy as jnp
        import numpy as np
        E = 8
        K = 2
        D = 256
        H = 512
        DOUT = 256
        EPS = 1e-05
        mu = jnp.mean(x, axis=-1, keepdims=True)
        var = jnp.mean(jnp.square(x - mu), axis=-1, keepdims=True)
        xn = (x - mu) * jax.lax.rsqrt(var + EPS) * gamma + beta
        logits = jnp.einsum('bsd,de->bse', xn, Wr) + br
        top_vals, top_idx = jax.lax.top_k(logits, K)
        w = jax.nn.softmax(top_vals, axis=-1)
        w_full = jnp.einsum('bsk,bske->bse', w, jax.nn.one_hot(top_idx, E, dtype=w.dtype))
        y = jnp.zeros(x.shape[:-1] + (DOUT,), x.dtype)
        for e in range(E):
            h = jax.nn.gelu(jnp.einsum('bsd,dh->bsh', xn, W1[e]) + b1[e], approximate=False)
            y_e = jnp.einsum('bsh,hd->bsd', h, W2[e]) + b2[e]
            y = y + y_e * w_full[..., e, None]
        return y

    def _L3_gnn_ref(x, edge_index, w1, b1, gamma, beta, w2, b2, w_gcn, b_gcn):
        import jax, jax.numpy as jnp
        import numpy as np
        N_NODES = 50000
        N_EDGES = 25000
        D_IN = 256
        D_OUT = 256
        BN_EPS = 1e-05

        def _forward(x, edge_index, w1, b1, gamma, beta, w2, b2, w_gcn, b_gcn):
            n = x.shape[0]
            h = x @ w1.T + b1
            mean = jnp.mean(h, axis=0)
            var = jnp.var(h, axis=0)
            h = (h - mean) * jax.lax.rsqrt(var + BN_EPS) * gamma + beta
            h = jax.nn.relu(h)
            h = h @ w2.T + b2
            xw = h @ w_gcn.T
            src = jnp.concatenate([edge_index[0], jnp.arange(n, dtype=edge_index.dtype)])
            dst = jnp.concatenate([edge_index[1], jnp.arange(n, dtype=edge_index.dtype)])
            deg = jax.ops.segment_sum(jnp.ones_like(dst, dtype=xw.dtype), dst, num_segments=n)
            dinv = jnp.where(deg > 0, jax.lax.rsqrt(jnp.maximum(deg, 1.0)), 0.0)
            norm = dinv[src] * dinv[dst]
            msgs = xw[src] * norm[:, None]
            out = jax.ops.segment_sum(msgs, dst, num_segments=n) + b_gcn
            return out
        return _forward(x, edge_index, w1, b1, gamma, beta, w2, b2, w_gcn, b_gcn)

    def _L3_ffn_ref(x, Wg, bg, W1, b1, W2, b2):
        import jax, jax.numpy as jnp
        import numpy as np
        B, S, D, E, H, K = (4, 128, 256, 8, 512, 2)
        Bv, Sv, Dv = x.shape
        gate_scores = x @ Wg + bg
        _, idx = jax.lax.top_k(gate_scores, K)
        mask = jax.nn.one_hot(idx, E, dtype=x.dtype).sum(axis=-2)
        xf = x.reshape(-1, Dv)
        mf = mask.reshape(-1, E)
        h = jax.nn.gelu(jnp.einsum('td,edh->teh', xf, W1) + b1[None], approximate=False)
        y = jnp.einsum('teh,ehd->ted', h, W2) + b2[None]
        out = jnp.einsum('ted,te->td', y, mf)
        return out.reshape(Bv, Sv, Dv)
    edge_index = jnp.stack([src, dst])
    deg = jnp.maximum(jax.ops.segment_sum(jnp.ones(dst.shape, jnp.float32), dst, num_segments=3125), 1.0)
    deg_isqrt = deg ** (-0.5)
    x = x + _L0_gnn_ref(_layernorm(x, axis=-1), L0_gnn_W, L0_gnn_attn, src, dst)
    x = x + _L0_ffn_ref(_layernorm(x, axis=-1)[None], L0_ffn_gate_w, L0_ffn_gate_b, L0_ffn_w1, L0_ffn_b1, L0_ffn_w2, L0_ffn_b2)[0]
    x = x + _L1_gnn_ref(_layernorm(x, axis=-1), edge_index, L1_gnn_W1, L1_gnn_b1, L1_gnn_W2, L1_gnn_b2, L1_gnn_wa1, L1_gnn_ba1, L1_gnn_wa2, L1_gnn_ba2)
    x = x + _L1_ffn_ref(_layernorm(x, axis=-1)[None], L1_ffn_Wg, L1_ffn_bg, L1_ffn_W1, L1_ffn_b1, L1_ffn_W2, L1_ffn_b2)[0]
    x = x + _L2_gnn_ref(_layernorm(x, axis=-1), deg_isqrt[:, None], L2_gnn_W, L2_gnn_b, src, dst)
    x = x + _L2_ffn_ref(_layernorm(x, axis=-1)[None], L2_ffn_gamma, L2_ffn_beta, L2_ffn_Wr, L2_ffn_br, L2_ffn_W1, L2_ffn_b1, L2_ffn_W2, L2_ffn_b2)[0]
    x = x + _L3_gnn_ref(_layernorm(x, axis=-1), edge_index, L3_gnn_w1, L3_gnn_b1, L3_gnn_gamma, L3_gnn_beta, L3_gnn_w2, L3_gnn_b2, L3_gnn_w_gcn, L3_gnn_b_gcn)
    x = x + _L3_ffn_ref(_layernorm(x, axis=-1)[None], L3_ffn_Wg, L3_ffn_bg, L3_ffn_W1, L3_ffn_b1, L3_ffn_W2, L3_ffn_b2)[0]
    return x

_drawn_inputs = setup_inputs


def setup_inputs(seed=0):
    import zlib

    import numpy as np

    out = dict(_drawn_inputs(seed))
    spreads = {'L0_ffn_gate_b': (0.0, 0.1),
     'L0_ffn_b1': (0.0, 0.635),
     'L0_ffn_b2': (0.0, 0.446),
     'L2_ffn_br': (0.0, 0.692),
     'L3_gnn_gamma': (1.0, 0.6),
     'L3_gnn_beta': (0.0, 2.0),
     'L3_gnn_b_gcn': (0.0, 1.053),
     'L3_ffn_bg': (0.0, 0.877),
     'L3_ffn_b1': (0.0, 2.0),
     'L3_ffn_b2': (0.0, 0.8)}
    factors = {'L1_gnn_b1': 5.906,
     'L1_ffn_bg': 6.64,
     'L1_ffn_b1': 8.0,
     'L1_ffn_b2': 8.0,
     'L2_gnn_b': 8.0,
     'L2_ffn_gamma': 8.0,
     'L2_ffn_beta': 8.0,
     'L2_ffn_Wr': 5.033,
     'L2_ffn_W1': 4.313,
     'L2_ffn_b1': 31.266,
     'L2_ffn_W2': 4.156,
     'L2_ffn_b2': 42.994,
     'L3_gnn_w1': 28.2,
     'L3_gnn_b1': 64.0,
     'L3_gnn_b2': 30.576,
     'L3_ffn_Wg': 2.714,
     'L3_ffn_W1': 5.986}
    for name, (base, spread) in spreads.items():
        noise = np.random.default_rng([zlib.crc32(name.encode()), seed]).standard_normal(out[name].shape)
        drawn = base * np.exp(spread * noise) if base else spread * noise
        out[name] = jnp.asarray(drawn.astype(out[name].dtype))
    for name, factor in factors.items():
        out[name] = (out[name] * factor).astype(out[name].dtype)
    return out
```

```python
from contextlib import ExitStack

import concourse.bass as bass
import concourse.mybir as mybir

ALU = mybir.AluOpType
ACT = mybir.ActivationFunctionType
AX = mybir.AxisListType.X
F32 = mybir.dt.float32
I32 = mybir.dt.int32

N = 3125
P = 125
T = N // P
U = 5
G = T // U
D = 256
H = D // 128
EDGES = 50000
HEADS = 4
HD = D // HEADS
EXPERTS = 8
SLOTS = 128
FAR = 1e30
BIG = 3.0e38
EPS = 1e-5

SLOT = [0, 1, 2, 0, 1]
BACK = [2, 2, 5, 3, 3]

RANGES = [(0, 13, [4, 3, 3, 3]), (13, 12, [3, 3, 3, 3])]


class Phase:

    def __init__(self, nc, name):
        self.nc, self.name, self.sems, self.ctx = nc, name, [], ExitStack()

    def __enter__(self):
        return self

    def sb(self, name, shape, dt=F32):
        return self.ctx.enter_context(self.nc.sbuf_tensor(f"{self.name}_{name}", shape, dt))

    def ps(self, name, shape=(128, 512)):
        return self.ctx.enter_context(self.nc.psum_tensor(f"{self.name}_{name}", list(shape), F32))

    def sem(self, name):
        s = self.nc.alloc_semaphore(f"{self.name}_{name}")
        self.sems.append(s)
        return s

    def __exit__(self, *error):
        self.ctx.close()
        if error[0] is None:
            self.nc.clear_and_free_semaphores(self.sems)
            self.nc.all_engine_barrier()


def turns(eng, body, last=G):
    body(0)
    with eng.Fori(1, last - 1) as g:
        body(g)
    body(last - 1)


def bcast(row, parts):
    return bass.AP(tensor=row.tensor, offset=row.offset, ap=[[0, parts]] + [list(x) for x in row.ap])


class Kernel:
    def __init__(self, nc, inp, out):
        self.nc, self.inp, self.out = nc, inp, out
        self.ctx = ExitStack()

        def dram(name, shape):
            return nc.dram_tensor(name, shape, F32, kind="Internal").ap()

        self.adj = dram("adj", [N * N + P, 1])
        self.adj2 = self.adj[0:N * N, :].rearrange("(s d) o -> s (d o)", s=N)
        self.adjT = dram("adjT", [N, N])
        self.xres = dram("xres", [N + SLOTS, D])
        self.xn = dram("xn", [N, D])
        self.feat = dram("feat", [N, HEADS * (HD + 1)])
        self.rows_a = dram("rows_a", [HEADS, N])
        self.rows_bm = dram("rows_bm", [2 * HEADS, N])
        self.row_a1 = dram("row_a1", [1, N])

        def sb(name, shape, dt=F32):
            return self.ctx.enter_context(nc.sbuf_tensor(name, shape, dt))

        self.ident = sb("ident", [128, 128])
        self.norm = sb("norm", [P, T])
        self.norm_self = sb("norm_self", [P, T])
        self.upto = sb("upto", [P, P])
        self.ones = sb("ones", [P, P])
        self.count = sb("count", [128, 128])
        self.rev = sb("rev", [P, EXPERTS])
        self.node = sb("node", [P, 2, T])
        self.dump = sb("dump", [SLOTS, 2])
        self.deg = sb("deg", [P, T])
        self.a_src = sb("a_src", [P, HEADS, T])
        self.b_dst = sb("b_dst", [P, HEADS, T])
        self.a2 = sb("a2", [P, T])
        nb = 56
        self.gidx = sb("gidx", [SLOTS, nb], I32)
        self.sidx = sb("sidx", [SLOTS, nb], I32)
        self.wslot = sb("wslot", [SLOTS, nb])
        self.eblk = sb("eblk", [1, nb], I32)


def tiles_of(x):
    return x.rearrange("(t p) d -> p t d", p=P)


def count_edges(K):
    nc = K.nc
    COLS = EDGES // P
    CH = 25
    NCH = COLS // CH
    AP_ = 100
    src_r = K.inp["src"].rearrange("(a x) -> a x", a=NCH)
    dst_r = K.inp["dst"].rearrange("(a x) -> a x", a=NCH)
    src_c = K.inp["src"].rearrange("(a x) -> a x", a=AP_)
    dst_c = K.inp["dst"].rearrange("(a x) -> a x", a=AP_)
    B = COLS // AP_
    with Phase(nc, "cnt") as ph:
        zero = ph.sb("zero", [P, N])
        sc = ph.sb("sc", [AP_, B * P], I32)
        dc = ph.sb("dc", [AP_, B * P], I32)
        cf = ph.sb("cf", [AP_, B * P])
        df = ph.sb("df", [AP_, B * P])
        col = ph.sb("col", [P, AP_, B])
        srow = ph.sb("srow", [P, 2, CH * P], I32)
        drow = ph.sb("drow", [P, 2, CH * P], I32)
        row = ph.sb("row", [P, CH * P])
        order = ph.sb("order", [P, P])
        junk = ph.sb("junk", [P, CH * P])
        lane = ph.sb("lane", [P, 1])
        total = ph.sb("total", [P, 2, CH])
        twin = ph.sb("twin", [P, CH])
        away = ph.sb("away", [P, CH])
        where = ph.sb("where", [P, 2, CH], I32)
        tp = [ph.ps(f"tp{b}") for b in range(B)]
        made = ph.sem("made")
        zeroed = ph.sem("zeroed")
        loaded = ph.sem("loaded")
        turned = ph.sem("turned")
        rows_in = [ph.sem(f"rows_in{s}") for s in range(2)]
        row_made = ph.sem("row_made")
        step = ph.sem("step")
        batch = ph.sem("batch")
        added = ph.sem("added")
        passed = ph.sem("passed")
        with nc.Block() as block:

            @block.sync
            def _(e):
                e.dma_start(sc[:], src_c).then_inc(loaded, 16)
                e.dma_start(dc[:], dst_c).then_inc(loaded, 16)
                e.wait_ge(made, 5)
                for i in range(T):
                    e.dma_start(K.adj2[i * P:(i + 1) * P, :], zero[:]).then_inc(zeroed, 16)
                e.dma_start(K.adj[N * N:N * N + P, :], zero[:, 0:1]).then_inc(zeroed, 16)
                e.dma_start(K.xres[0:N, :].rearrange("(a b) d -> a (b d)", a=T), K.inp["x"].rearrange("(a b) d -> a (b d)", a=T)).then_inc(zeroed, 16)
                e.dma_start(K.xres[N:N + P, :], zero[:, 0:D]).then_inc(zeroed, 16)
                e.dma_start(K.xres[N + P:N + SLOTS, :], zero[0:SLOTS - P, 0:D]).then_inc(zeroed, 16)
                e.wait_ge(zeroed, 16 * (T + 4))

            @block.scalar
            def _(e):
                def load(g):
                    for s in range(2):
                        if not isinstance(g, int) or g > 0:
                            e.wait_ge(row_made, 2 * (2 * g + s) - 2)
                        e.dma_start(srow[:, s, :], bcast(src_r[bass.ds(2 * g + s, 1), :].rearrange("a x -> (a x)"), P)).then_inc(rows_in[s], 16)
                        e.dma_start(drow[:, s, :], bcast(dst_r[bass.ds(2 * g + s, 1), :].rearrange("a x -> (a x)"), P)).then_inc(rows_in[s], 16)
                load(0)
                with e.Fori(1, NCH // 2) as g:
                    load(g)

            @block.tensor
            def _(e):
                e.wait_ge(loaded, 33)
                e.wait_ge(made, 5)
                for b in range(B):
                    e.transpose(tp[b][0:P, 0:AP_], cf[:, b * P:(b + 1) * P], K.ident[0:AP_, 0:AP_]).then_inc(turned, 1)

            @block.vector
            def _(e):
                e.memset(zero[:], 0.0).then_inc(made, 1)
                e.wait_ge(loaded, 32)
                e.tensor_copy(df[:], dc[:]).then_inc(step, 1)
                e.wait_ge(step, 1)
                e.scalar_tensor_tensor(out=cf[:], in0=sc[:], scalar=float(N), in1=df[:], op0=ALU.mult, op1=ALU.add).then_inc(loaded, 1)
                e.wait_ge(turned, B)
                for b in range(B):
                    e.tensor_copy(col[:, :, b], tp[b][0:P, 0:AP_]).then_inc(step, 1)
                e.wait_ge(step, 1 + B)
                e.wait_ge(made, 5)
                cols = col[:].rearrange("p a b -> p (a b)")

                def chunk(g, s):
                    c = 2 * g + s
                    e.wait_ge(rows_in[s], 32 * g + 32)
                    e.tensor_scalar(row[:], srow[:, s, :], float(N), None, ALU.mult).then_inc(row_made, 1)
                    e.wait_ge(row_made, 2 * c + 1)
                    e.tensor_tensor(row[:], row[:], drow[:, s, :], ALU.add).then_inc(row_made, 1)
                    e.wait_ge(row_made, 2 * c + 2)
                    if (not isinstance(g, int) or g > 0):
                        e.wait_ge(added, 16 * CH * (c - 1))
                    for i in range(CH):
                        last = e.scalar_tensor_tensor(out=junk[:, i * P:(i + 1) * P], in0=row[:, i * P:(i + 1) * P],
                                                      scalar=cols[:, bass.ds(c * CH + i, 1)],
                                                      in1=order[:], op0=ALU.is_equal, op1=ALU.mult, accum_out=total[:, s, i:i + 1])
                    last.then_inc(step, 1)
                    e.wait_ge(step, 1 + B + 4 * c + 1)
                    e.tensor_scalar(twin[:], total[:, s, :], 1024.0, None, ALU.is_ge).then_inc(step, 1)
                    mine = cols[:, bass.ds(c * CH, CH)]
                    e.tensor_scalar(away[:], mine, -1.0, lane[:, 0:1], ALU.mult, ALU.add).then_inc(step, 1)
                    e.wait_ge(step, 1 + B + 4 * c + 3)
                    e.tensor_tensor(away[:], away[:], twin[:], ALU.mult).then_inc(step, 1)
                    e.wait_ge(step, 1 + B + 4 * c + 4)
                    e.tensor_tensor(where[:, s, :], away[:], mine, ALU.add).then_inc(batch, 1)

                chunk(0, 0)
                chunk(0, 1)
                with e.Fori(1, NCH // 2) as g:
                    chunk(g, 0)
                    chunk(g, 1)

            @block.gpsimd
            def _(e):
                e.memset(K.ident[:], 0.0).then_inc(made, 1)
                e.memset(order[:], 1.0).then_inc(made, 1)
                e.wait_ge(made, 3)
                e.affine_select(out=K.ident[:], in_=K.ident[:], compare_op=ALU.not_equal, fill=1.0, base=0,
                                pattern=[[-1, 128]], channel_multiplier=1)
                e.affine_select(out=order[:], in_=order[:], compare_op=ALU.is_ge, fill=1025.0, base=0,
                                pattern=[[1, P]], channel_multiplier=-1).then_inc(made, 1)
                approx = dict(allow_small_or_imprecise_dtypes=True)
                e.memset(K.upto[:], 1.0).then_inc(passed, 1)
                e.memset(K.ones[:], 1.0)
                e.iota(K.count[:], pattern=[[1, 128]], base=0, channel_multiplier=0, **approx)
                e.iota(K.rev[:], pattern=[[-1, EXPERTS]], base=EXPERTS, channel_multiplier=0, **approx)
                e.iota(K.node[:], pattern=[[0, 2], [P, T]], base=0, channel_multiplier=1, **approx)
                e.iota(K.dump[:, 0:1], pattern=[[0, 1]], base=N, channel_multiplier=1, **approx)
                e.iota(K.dump[:, 1:2], pattern=[[0, 1]], base=-N, channel_multiplier=-1, **approx)
                e.wait_ge(passed, 1)
                e.affine_select(out=K.upto[:], in_=K.upto[:], compare_op=ALU.is_ge, fill=0.0, base=0,
                                pattern=[[1, P]], channel_multiplier=-1)
                e.iota(lane[:], pattern=[[0, 1]], base=N * N, channel_multiplier=1,
                       allow_small_or_imprecise_dtypes=True).then_inc(made, 1)
                bound = e.to_reg(N * N + P - 1)
                e.wait_ge(zeroed, 16 * (T + 4))

                def add(g):
                    for s in range(2):
                        e.wait_ge(batch, 2 * g + s + 1)
                        e.sem_inc(passed, 1)
                        for i in range(CH):
                            n = (2 * g + s) * CH + i
                            if not isinstance(n, int) or n > 0:
                                e.wait_ge(added, 16 * n)
                                e.sem_inc(passed, 1)
                            e.indirect_dma_start(K.adj, bass.IndirectOffsetOnAxis(ap=where[:, s, i:i + 1], axis=0),
                                                 total[:, s, i:i + 1], None, bounds_check=bound,
                                                 oob_is_err=True, compute_op=ALU.add).then_inc(added, 16)
                add(0)
                with e.Fori(1, NCH // 2) as g:
                    add(g)
                e.wait_ge(added, 16 * COLS)


class Chain:

    def __init__(self, eng, sem):
        self.eng, self.sem, self.n = eng, sem, 0

    def __call__(self, ins):
        self.n += 1
        ins.then_inc(self.sem, 1)

    def settle(self):
        self.eng.wait_ge(self.sem, self.n)


def node_stats(e, link, x, st, mean, rstd, sq, diff, vector, power):
    def stats(t):
        return vector.bn_stats(st[:, t, :], x[:, t, :])
    for t in range(T):
        link(stats(t))
    link.settle()
    me, mo, se, so = (st[:, :, i] for i in (1, 4, 2, 5))
    link(vector.tensor_tensor(mean[:], me, mo, ALU.add))
    link(vector.tensor_tensor(diff[:], me, mo, ALU.subtract))
    link(vector.tensor_tensor(rstd[:], se, so, ALU.add))
    link.settle()
    link(vector.tensor_tensor(sq[:], diff[:], diff[:], ALU.mult))
    link(vector.tensor_scalar(mean[:], mean[:], 0.5, None, ALU.mult))
    link(vector.tensor_scalar(rstd[:], rstd[:], 1.0 / D, EPS, ALU.mult, ALU.add))
    link.settle()
    link(vector.scalar_tensor_tensor(out=rstd[:], in0=sq[:], scalar=0.25, in1=rstd[:], op0=ALU.mult, op1=ALU.add))
    link.settle()
    inverse_root(e, link, rstd, sq, diff, power)


def inverse_root(e, link, x, root, tmp, power):
    asked, given, n = power
    e.sem_inc(asked, 1)
    e.wait_ge(given, n)
    link(e.reciprocal(root[:], root[:]))
    link.settle()
    link(e.tensor_tensor(tmp[:], root[:], root[:], ALU.mult))
    link.settle()
    link(e.tensor_tensor(tmp[:], tmp[:], x[:], ALU.mult))
    link.settle()
    link(e.tensor_scalar(tmp[:], tmp[:], -0.5, 1.5, ALU.mult, ALU.add))
    link.settle()
    link(e.tensor_tensor(x[:], tmp[:], root[:], ALU.mult))
    link.settle()


def root_of(e, power, root, x):
    asked, given, n = power
    e.wait_ge(asked, n)
    e.activation(root[:], x[:], ACT.Sqrt).then_inc(given, 1)


def load_x(e, K, x, x_in):
    for g in range(G):
        e.dma_start(x[:, g * U:(g + 1) * U, :], tiles_of(K.xres[0:N, :])[:, g * U:(g + 1) * U, :]).then_inc(x_in, 16)


def rows_from(e_pe, K, src, cols, ps, done):
    e_pe.transpose(ps[0:cols, 0:P], src, K.ident[0:P, 0:P]).then_inc(done, 1)


def project(K, layer, w, M, bias, finish_steps):
    nc = K.nc
    with Phase(nc, f"proj{layer}") as ph:
        x = ph.sb("x", [P, T, D])
        y = ph.sb("y", [P, T, M])
        st = ph.sb("st", [P, T, 6])
        mean, rstd, sq, diff = (ph.sb(n, [P, T]) for n in ("mean", "rstd", "sq", "diff"))
        xn = ph.sb("xn", [P, 3, D])
        xT = ph.sb("xT", [128, 3, H, P])
        wsb = ph.sb("w", [128, H, M])
        bsb = ph.sb("b", [P, M])
        xT_ps = [ph.ps(f"xTp{i}") for i in range(3)]
        y_ps = [ph.ps(f"yp{i}") for i in range(3)]
        row_ps = [ph.ps(f"rp{i}") for i in range(2)]
        F = finish_steps(K, ph)
        x_in, w_in = ph.sem("x_in"), ph.sem("w_in")
        xn_made, turned, xT_made, y_sum, y_made, step = (ph.sem(n) for n in ("xn_made", "turned", "xT_made", "y_sum", "y_made", "step"))
        finished, row_turned, row_made, stored = (ph.sem(n) for n in ("finished", "row_turned", "row_made", "stored"))
        base = {}
        power = (ph.sem("var_ready"), ph.sem("rstd_ready"), 1)
        with nc.Block() as block:

            @block.sync
            def _(e):
                load_x(e, K, x, x_in)
                e.dma_start(wsb[:], w).then_inc(w_in, 16)
                n = 1
                if bias is not None:
                    e.dma_start(bsb[:], bcast(bias, P)).then_inc(w_in, 16)
                    n += 1
                for dst, src in F.get("loads", []):
                    e.dma_start(dst, src).then_inc(w_in, 16)
                    n += 1
                e.wait_ge(finished, 1)
                k = 0
                for dst, src in F["stores"](x, y):
                    e.dma_start(dst, src).then_inc(stored, 16)
                    k += 1
                if F.get("rows"):
                    e.wait_ge(row_made, 1)
                    for dst, src in F["row_stores"]:
                        e.dma_start(dst, src).then_inc(stored, 16)
                        k += 1
                e.wait_ge(stored, 16 * k)

            base["w"] = 16 * (1 + (bias is not None) + len(F.get("loads", [])))

            @block.tensor
            def _(e):
                e.wait_ge(w_in, base["w"])

                def body(g):
                    for k in range(U):
                        t = g * U + k
                        s = SLOT[k]
                        e.wait_ge(xn_made, t + 1)
                        if not isinstance(t, int) or t >= BACK[k]:
                            if not (isinstance(t, int) and t < 3):
                                e.wait_ge(xT_made, t - BACK[k] + 1)
                        for h in range(H):
                            ins = e.transpose(xT_ps[s][:, h * P:(h + 1) * P], xn[:, s, h * 128:(h + 1) * 128], K.ident[0:P, 0:P])
                        ins.then_inc(turned, 1)
                        e.wait_ge(xT_made, t + 1)
                        if not (isinstance(t, int) and t < 3):
                            e.wait_ge(y_made, t - BACK[k] + 1)
                        for h in range(H):
                            ins = e.matmul(y_ps[s][0:P, 0:M], xT[:, s, h, :], wsb[:, h, :], start=h == 0, stop=h == H - 1)
                        ins.then_inc(y_sum, 1)
                turns(e, body)
                if F.get("rows"):
                    src, cols = F["rows"]
                    e.wait_ge(finished, 1)
                    e.transpose(row_ps[0][0:cols, 0:P], src, K.ident[0:P, 0:P]).then_inc(row_turned, 1)

            @block.scalar
            def _(e):
                root_of(e, power, sq, rstd)

                def body(g):
                    for k in range(U):
                        t = g * U + k
                        s = SLOT[k]
                        e.wait_ge(turned, t + 1)
                        if not (isinstance(t, int) and t < 3):
                            e.wait_ge(y_sum, t - BACK[k] + 1)
                        e.copy(xT[:, s, :, :].rearrange("p h n -> p (h n)"), xT_ps[s][:, 0:H * P]).then_inc(xT_made, 1)
                turns(e, body)

            @block.vector
            def _(e):
                link = Chain(e, step)
                e.wait_ge(x_in, 16 * G)
                node_stats(e, link, x, st, mean, rstd, sq, diff, e, power)
                e.wait_ge(w_in, base["w"])

                def normalise(g, k):
                    t = g * U + k
                    if not (isinstance(t, int) and t < 3):
                        e.wait_ge(turned, t - BACK[k] + 1)
                        if added is not None:
                            e.wait_ge(added, t - BACK[k] + 1)
                    e.tensor_scalar(xn[:, SLOT[k], :], x[:, bass.ds(t, 1), :].rearrange("p a d -> p (a d)"), mean[:, bass.ds(t, 1)], rstd[:, bass.ds(t, 1)],
                                    ALU.subtract, ALU.mult).then_inc(xn_made, 1)

                def collect(g, k):
                    t = g * U + k
                    e.wait_ge(y_sum, t + 1)
                    o = y[:, bass.ds(t, 1), :].rearrange("p a d -> p (a d)")
                    if bias is None:
                        e.tensor_copy(o, y_ps[SLOT[k]][0:P, 0:M]).then_inc(y_made, 1)
                    else:
                        e.tensor_tensor(o, y_ps[SLOT[k]][0:P, 0:M], bsb[:], ALU.add).then_inc(y_made, 1)
                    if F.get("add_xn"):
                        xt = x[:, bass.ds(t, 1), :].rearrange("p a d -> p (a d)")
                        e.wait_ge(xn_made, t + 1)
                        e.tensor_tensor(xt, xt, xn[:, SLOT[k], :], ALU.add).then_inc(added, 1)

                added = ph.sem("added") if F.get("add_xn") else None

                def body(g):
                    for k in range(U):
                        normalise(g, k)
                        if k >= 1:
                            collect(g, k - 1)
                    collect(g, U - 1)
                turns(e, body)
                e.wait_ge(y_made, T)
                if added is not None:
                    e.wait_ge(added, T)
                F["finish"](e, link, y)
                link.settle()
                e.sem_inc(finished, 1)
                if F.get("rows"):
                    src, cols = F["rows"]
                    e.wait_ge(row_turned, 1)
                    e.tensor_copy(F["rows_sb"][0:cols, :], row_ps[0][0:cols, 0:P]).then_inc(row_made, 1)


def project_attention(K):
    def steps(K, ph):
        tmp = ph.sb("tmp", [P, T, D])
        feat = ph.sb("feat", [P, T, HEADS, HD + 1])
        att = ph.sb("att", [P, 2, HD])
        rows = ph.sb("rows", [HEADS * T, P])

        def finish(e, link, y):
            link(e.memset(feat[:, :, :, HD:HD + 1], 1.0))
            for i, into in enumerate((K.a_src, K.b_dst)):
                for h in range(HEADS):
                    link(e.tensor_tensor(tmp[:, :, h * HD:(h + 1) * HD], y[:, :, h * HD:(h + 1) * HD],
                                         att[:, i:i + 1, :].broadcast_to([P, T, HD]), ALU.mult))
                link.settle()
                for h in range(HEADS):
                    link(e.tensor_reduce(into[:, h, :], tmp[:, :, h * HD:(h + 1) * HD], AX, ALU.add))
                link.settle()
            for h in range(HEADS):
                link(e.tensor_copy(feat[:, :, h, 0:HD], y[:, :, h * HD:(h + 1) * HD]))

        return dict(
            loads=[(att[:], bcast(K.inp["L0_gnn_attn"][0:1, :].rearrange("a (i d) -> (a i) d", i=2), P))],
            finish=finish,
            stores=lambda x, y: [(tiles_of(K.feat), feat[:].rearrange("p t h d -> p t (h d)"))],
            rows=(K.a_src[:].rearrange("p h t -> p (h t)"), HEADS * T), rows_sb=rows,
            row_stores=[(K.rows_a.rearrange("h (t p) -> (h t) p", p=P), rows[:])],
        )
    project(K, 0, K.inp["L0_W"], D, None, steps)


def neighbour_maxima(K):
    nc = K.nc
    NB = 7
    with Phase(nc, "max") as ph:
        strip = ph.sb("strip", [P, 3, T, P])
        turned_sb = ph.sb("turned", [P, 3, N])
        a_row = ph.sb("a_row", [P, HEADS, N])
        gone = ph.sb("gone", [P, N])
        junk = ph.sb("junk", [P, N])
        top = ph.sb("top", [P, HEADS, T])
        top_j = ph.sb("top_j", [P, U, HEADS])
        degp = ph.sb("degp", [P, T, NB])
        m, t1, t2 = (ph.sb(n, [P, HEADS, T]) for n in ("m", "t1", "t2"))
        bm = ph.sb("bm", [P, 2, HEADS, T])
        rows = ph.sb("rows", [HEADS * T, 2, P])
        ps = [ph.ps(f"p{i}") for i in range(NB)]
        strip_in = [ph.sem(f"strip_in{s}") for s in range(U)]
        a_in, bank_full, bank_copied, gone_made, top_made, strip_step, step = (
            ph.sem(n) for n in ("a_in", "bank_full", "bank_copied", "gone_made", "top_made", "strip_step", "step"))
        kept = [ph.sem(f"kept{k}") for k in range(U)]
        row_turned, row_made, stored, mask_step, ready = (ph.sem(n) for n in ("row_turned", "row_made", "stored", "mask_step", "ready"))
        top_put = ph.sem("top_put")
        root, tmp = ph.sb("root", [P, T]), ph.sb("tmp", [P, T])
        asked, given = ph.sem("asked"), ph.sem("given")
        widths = [min(4, T - 4 * b) for b in range(NB)]
        adj3 = K.adj2.rearrange("(t p) d -> p t d", p=P)
        with nc.Block() as block:

            @block.sync
            def _(e):
                for h in range(HEADS):
                    e.dma_start(a_row[:, h, :], bcast(K.rows_a[h], P)).then_inc(a_in, 16)

                def body(g):
                    for k in range(U):
                        j = g * U + k
                        if not (isinstance(j, int) and j < 3):
                            e.wait_ge(bank_full, NB * (j - BACK[k] + 1))
                        e.dma_start(strip[:, SLOT[k], :, :], adj3[:, :, bass.ds(j * P, P)]).then_inc(strip_in[k], 16)
                turns(e, body)
                e.wait_ge(row_made, 2)
                for i in range(2):
                    e.dma_start(K.rows_bm[i * HEADS:(i + 1) * HEADS, :].rearrange("h (t p) -> (h t) p", p=P), rows[:, i, :]).then_inc(stored, 16)
                e.wait_ge(stored, 32)

            @block.tensor
            def _(e):
                def body(g):
                    for k in range(U):
                        j = g * U + k
                        e.wait_ge(strip_in[k], 16 * g + 16)
                        for b in range(NB):
                            if not (isinstance(j, int) and j < 1):
                                e.wait_ge(bank_copied, NB * (j - 1) + b + 1)
                            for i in range(widths[b]):
                                ins = e.transpose(ps[b][0:P, i * P:(i + 1) * P], strip[:, SLOT[k], 4 * b + i, :], K.ident[0:P, 0:P])
                            ins.then_inc(bank_full, 1)
                turns(e, body)
                e.wait_ge(ready, 1)
                e.wait_ge(bank_copied, NB * T)
                for i in range(2):
                    e.transpose(ps[i][0:HEADS * T, 0:P], bm[:, i, :, :].rearrange("p h t -> p (h t)"), K.ident[0:P, 0:P]).then_inc(row_turned, 1)

            @block.scalar
            def _(e):
                def body(g):
                    for k in range(U):
                        j = g * U + k
                        if not (isinstance(j, int) and j < 3):
                            e.wait_ge(top_made, HEADS * (j - BACK[k] + 1))
                            kb = (k - BACK[k]) % U
                            gb = g if k - BACK[k] >= 0 else g - 1
                            e.wait_ge(kept[kb], 16 * gb + 16)
                        for b in range(NB):
                            e.wait_ge(bank_full, NB * j + b + 1)
                            e.activation(turned_sb[:, SLOT[k], 4 * b * P:4 * b * P + widths[b] * P], ps[b][0:P, 0:widths[b] * P],
                                         ACT.Copy, accum_out=degp[:, bass.ds(j, 1), b]).then_inc(bank_copied, 1)
                turns(e, body)
                root_of(e, (asked, given, 1), root, K.norm)
                root_of(e, (asked, given, 2), root, K.norm_self)

            @block.gpsimd
            def _(e):
                def body(g):
                    for k in range(U):
                        j = g * U + k
                        e.wait_ge(bank_copied, NB * (j + 1))
                        e.sem_inc(strip_step, 1)
                        e.dma_start(K.adjT[bass.ds(j * P, P), :], turned_sb[:, SLOT[k], :]).then_inc(kept[k], 16)
                turns(e, body)
                for k in range(U):
                    e.wait_ge(kept[k], 16 * G)

            @block.vector
            def _(e):
                link = Chain(e, step)
                e.wait_ge(a_in, 16 * HEADS)

                def body(g):
                    for k in range(U):
                        j = g * U + k
                        e.wait_ge(bank_copied, NB * (j + 1))
                        if not (isinstance(j, int) and j < 1):
                            e.wait_ge(top_made, HEADS * j)
                        e.tensor_scalar(gone[:], turned_sb[:, SLOT[k], :], 0.0, -FAR, ALU.is_equal, ALU.mult).then_inc(gone_made, 1)
                        e.wait_ge(gone_made, j + 1)
                        e.sem_inc(mask_step, 1)
                        for h in range(HEADS):
                            if h > 0:
                                e.wait_ge(top_made, HEADS * j + h)
                                e.sem_inc(mask_step, 1)
                            e.tensor_tensor_reduce(junk[:], gone[:], a_row[:, h, :], 1.0, -FAR, ALU.add, ALU.max,
                                                   top_j[:, k, h:h + 1]).then_inc(top_made, 1)
                        e.wait_ge(top_made, HEADS * (j + 1))
                        e.tensor_copy(top[:, :, bass.ds(j, 1)].rearrange("p h a -> p (h a)"), top_j[:, k, :]).then_inc(top_put, 1)
                turns(e, body)
                e.wait_ge(top_put, T)
                link(e.tensor_reduce(K.deg[:], degp[:], AX, ALU.add))
                link(e.tensor_tensor(t1[:], top[:], K.b_dst[:], ALU.add))
                link(e.tensor_scalar(t2[:], top[:], -0.5 * FAR, None, ALU.is_gt))
                link.settle()
                link(e.scalar_tensor_tensor(out=m[:], in0=t1[:], scalar=0.01, in1=t1[:], op0=ALU.mult, op1=ALU.max))
                link.settle()
                link(e.tensor_tensor(m[:], m[:], t2[:], ALU.mult))
                link.settle()
                link(e.tensor_tensor(bm[:, 0, :, :], K.b_dst[:], m[:], ALU.subtract))
                link(e.scalar_tensor_tensor(out=bm[:, 1, :, :], in0=K.b_dst[:], scalar=0.01, in1=m[:], op0=ALU.mult, op1=ALU.subtract))
                link.settle()
                e.sem_inc(ready, 1)
                link(e.tensor_scalar(K.norm[:], K.deg[:], 1.0, None, ALU.max))
                link(e.tensor_scalar(K.norm_self[:], K.deg[:], 1.0, None, ALU.add))
                link.settle()
                inverse_root(e, link, K.norm, root, tmp, (asked, given, 1))
                inverse_root(e, link, K.norm_self, root, tmp, (asked, given, 2))
                for i in range(2):
                    e.wait_ge(row_turned, i + 1)
                    e.tensor_copy(rows[:, i, :], ps[i][0:HEADS * T, 0:P]).then_inc(row_made, 1)


def aggregate(K, layer, passes, matrix, M, feat_cols, weigh=None, scale=None):
    nc = K.nc
    attention, sigmoid = weigh == "attention", weigh == "sigmoid"
    WMAX = 13 * P
    with Phase(nc, f"agg{layer}") as ph:
        block_sb = ph.sb("block", [P, 3, WMAX])
        feat = ph.sb("feat", [P, 3, 2 * M])
        if weigh:
            wgt = ph.sb("wgt", [P, 3, 2 if attention else 1, WMAX])
        if attention:
            low = ph.sb("low", [P, 3, 2, WMAX])
            rows = ph.sb("rows", [P, 2, 2, WMAX])
            a_low = ph.sb("a_low", [P, HEADS, T])
            den = ph.sb("den", [P, 13, 2])
            part = ph.sb("part", [P, 13, 2, HD])
        if sigmoid:
            rows = ph.sb("rows", [P, 2, WMAX])
        xw = 2 * HD if attention else D
        sums = ph.sb("sums", [M, 2, WMAX])
        x = ph.sb("x", [P, 13, xw])
        ps = [ph.ps(f"p{i}") for i in range(8)]
        block_in = [ph.sem(f"block_in{k}") for k in range(U)]
        rows_in, x_in, stored = ph.sem("rows_in"), ph.sem("x_in"), ph.sem("stored")
        used, summed, copied, tiled, x_made, rows_used = (ph.sem(n) for n in ("used", "summed", "copied", "tiled", "x_made", "rows_used"))
        exp_made, max_made, w_made, step = (ph.sem(n) for n in ("exp_made", "max_made", "w_made", "step"))
        NW = 2 if attention else 1
        per_bank = 3 if attention else 2
        row_dmas = 4 if attention else 1 if sigmoid else 0

        def geometry(q):
            first, count, chunks = RANGES[passes[q][0]]
            return first, count, chunks

        def x_rows(q):
            first, count, _ = geometry(q)
            v = tiles_of(K.xres[0:N, :])[:, first:first + count, :]
            return v[:, :, passes[q][1] * xw:(passes[q][1] + 1) * xw] if attention else v

        with nc.Block() as block:

            @block.sync
            def _(e):
                for q in range(len(passes)):
                    first, count, chunks = geometry(q)
                    if q > 0:
                        if row_dmas:
                            e.wait_ge(rows_used, q)
                        e.wait_ge(stored, 16 * q)
                    if attention:
                        hp = passes[q][1]
                        for i in range(2):
                            for v in range(2):
                                e.dma_start(rows[:, v, i, 0:count * P], bcast(K.rows_bm[v * HEADS + 2 * hp + i, first * P:(first + count) * P], P)).then_inc(rows_in, 16)
                    if sigmoid:
                        e.dma_start(rows[:, 0, 0:count * P], bcast(K.row_a1[0, first * P:(first + count) * P], P)).then_inc(rows_in, 16)
                    e.dma_start(x[:, 0:count, :], x_rows(q)).then_inc(x_in, 16)
                    fc = feat_cols(passes[q])

                    def body(g):
                        for k in range(U):
                            t = g * U + k
                            i = q * T + t
                            if not (isinstance(i, int) and i < 3):
                                e.wait_ge(used, i - BACK[k] + 1)
                            e.dma_start(block_sb[:, SLOT[k], 0:count * P], matrix[bass.ds(t * P, P), first * P:(first + count) * P]).then_inc(block_in[k], 16)
                            e.dma_start(feat[:, SLOT[k], :], K.feat[bass.ds(t * P, P), fc:fc + 2 * M]).then_inc(block_in[k], 16)
                    turns(e, body)
                    e.wait_ge(x_made, q + 1)
                    e.dma_start(x_rows(q), x[:, 0:count, :]).then_inc(stored, 16)
                e.wait_ge(stored, 16 * len(passes))

            @block.tensor
            def _(e):
                for q in range(len(passes)):
                    first, count, chunks = geometry(q)
                    if q > 0:
                        e.wait_ge(x_made, q)

                    def body(g):
                        for k in range(U):
                            t = g * U + k
                            s = SLOT[k]
                            e.wait_ge(block_in[k], 32 * (q * G + g) + 32)
                            for i in range(2):
                                if weigh and i < NW:
                                    e.wait_ge(w_made, NW * (q * T + t) + i + 1)
                                c0 = 0
                                for c in range(4):
                                    n = chunks[c] * P
                                    rhs = wgt[:, s, i % NW, c0:c0 + n] if weigh else block_sb[:, s, c0:c0 + n]
                                    ins = e.matmul(ps[4 * i + c][0:M, 0:n], feat[:, s, i * M:(i + 1) * M], rhs,
                                                   start=isinstance(t, int) and t == 0, stop=isinstance(t, int) and t == T - 1)
                                    c0 += n
                            ins.then_inc(used, 1)
                    turns(e, body)
                    e.wait_ge(copied, 8 * (q + 1))
                    for j in range(count):
                        b, o = j // per_bank, (j % per_bank) * 2 * M
                        for i in range(2):
                            ins = e.transpose(ps[b][0:P, o + i * M:o + (i + 1) * M], sums[:, i, j * P:(j + 1) * P], K.ident[0:M, 0:M])
                    ins.then_inc(tiled, 1)

            @block.scalar
            def _(e):
                if attention:
                    e.wait_ge(max_made, 1)
                for q in range(len(passes)):
                    first, count, chunks = geometry(q)
                    n = count * P
                    if weigh:
                        e.wait_ge(rows_in, 16 * row_dmas * (q + 1))

                        def body(g):
                            for k in range(U):
                                t = g * U + k
                                i = q * T + t
                                s = SLOT[k]
                                if not (isinstance(i, int) and i < 3):
                                    e.wait_ge(used, i - BACK[k] + 1)
                                if attention:
                                    hp = passes[q][1]
                                    for a in range(2):
                                        e.activation(wgt[:, s, a, 0:n], rows[:, 0, a, 0:n], ACT.Exp, bias=K.a_src[:, 2 * hp + a, bass.ds(t, 1)]).then_inc(exp_made, 1)
                                        e.activation(low[:, s, a, 0:n], rows[:, 1, a, 0:n], ACT.Exp, bias=a_low[:, 2 * hp + a, bass.ds(t, 1)]).then_inc(exp_made, 1)
                                else:
                                    e.activation(wgt[:, s, 0, 0:n], rows[:, 0, 0:n], ACT.Sigmoid, bias=K.a2[:, bass.ds(t, 1)]).then_inc(exp_made, 1)
                        turns(e, body)
                        e.wait_ge(exp_made, 2 * NW * T * (q + 1) if attention else T * (q + 1))
                        e.sem_inc(rows_used, 1)
                    e.wait_ge(used, T * (q + 1))
                    if q > 0:
                        e.wait_ge(tiled, q)
                    c0 = 0
                    for c in range(4):
                        w = chunks[c] * P
                        e.copy(sums[:, 0, c0:c0 + w], ps[c][0:M, 0:w]).then_inc(copied, 1)
                        c0 += w

            @block.vector
            def _(e):
                link = Chain(e, step)
                if attention:
                    e.tensor_scalar(a_low[:], K.a_src[:], 0.01, None, ALU.mult).then_inc(max_made, 1)
                for q in range(len(passes)):
                    first, count, chunks = geometry(q)
                    n = count * P

                    def body(g):
                        for k in range(U):
                            t = g * U + k
                            i = q * T + t
                            s = SLOT[k]
                            if attention:
                                for a in range(2):
                                    e.wait_ge(exp_made, 2 * (NW * i + a) + 2)
                                    e.tensor_tensor(wgt[:, s, a, 0:n], wgt[:, s, a, 0:n], low[:, s, a, 0:n], ALU.max).then_inc(max_made, 1)
                                e.wait_ge(block_in[k], 32 * (q * G + g) + 32)
                                for a in range(2):
                                    e.wait_ge(max_made, 1 + NW * i + a + 1)
                                    e.scalar_tensor_tensor(out=wgt[:, s, a, 0:n], in0=wgt[:, s, a, 0:n], scalar=BIG, in1=block_sb[:, s, 0:n],
                                                           op0=ALU.min, op1=ALU.mult).then_inc(w_made, 1)
                            else:
                                e.wait_ge(block_in[k], 32 * (q * G + g) + 32)
                                e.wait_ge(exp_made, i + 1)
                                e.tensor_tensor(wgt[:, s, 0, 0:n], wgt[:, s, 0, 0:n], block_sb[:, s, 0:n], ALU.mult).then_inc(w_made, 1)
                    if weigh:
                        turns(e, body)
                    e.wait_ge(used, T * (q + 1))
                    if q > 0:
                        e.wait_ge(tiled, q)
                    c0 = 0
                    for c in range(4):
                        w = chunks[c] * P
                        e.tensor_copy(sums[:, 1, c0:c0 + w], ps[4 + c][0:M, 0:w]).then_inc(copied, 1)
                        c0 += w
                    e.wait_ge(tiled, q + 1)
                    e.wait_ge(x_in, 16 * (q + 1))
                    if attention:
                        views = []
                        for b in range((count + 2) // 3):
                            m = min(3, count - 3 * b)
                            v = ps[b][0:P, 0:m * 2 * M].rearrange("p (j f) -> p j f", f=M)
                            views.append((b, m, v))
                            link(e.tensor_scalar(den[:, 3 * b:3 * b + m, :].rearrange("p j i -> p (j i)"), v[:, :, HD], 1e-9, None, ALU.max))
                        link.settle()
                        link(e.reciprocal(den[:, 0:count, :], den[:, 0:count, :]))
                        link.settle()
                        for b, m, v in views:
                            link(e.tensor_tensor(part[:, 3 * b:3 * b + m, :, :].rearrange("p j i f -> p (j i) f"), v[:, :, 0:HD],
                                                 den[:, 3 * b:3 * b + m, :].rearrange("p j (i a) -> p (j i) a", a=1).broadcast_to([P, 2 * m, HD]), ALU.mult))
                        link.settle()
                        e.tensor_tensor(x[:, 0:count, :], x[:, 0:count, :], part[:, 0:count, :, :].rearrange("p j i f -> p j (i f)"), ALU.add).then_inc(x_made, 1)
                    else:
                        for j in range(count):
                            v = ps[j // 2][0:P, (j % 2) * D:(j % 2 + 1) * D]
                            ins = e.scalar_tensor_tensor(out=x[:, j, :], in0=v, scalar=1.0 if scale is None else scale[:, first + j:first + j + 1], in1=x[:, j, :],
                                                         op0=ALU.mult, op1=ALU.add)
                        ins.then_inc(x_made, 1)


def attend(K):
    passes = [(r, hp) for hp in range(2) for r in range(2)]
    aggregate(K, 0, passes, K.adj2, HD + 1, lambda p: p[1] * 2 * (HD + 1), "attention")


def project_gate(K):
    def steps(K, ph):
        tmp = ph.sb("tmp", [P, T, D])
        wa = ph.sb("wa", [P, 2, D])
        ba = ph.sb("ba", [P, 2])
        a1 = ph.sb("a1", [P, T])
        rows = ph.sb("rows", [T, P])

        def finish(e, link, y):
            link(e.scalar_tensor_tensor(out=y[:], in0=y[:], scalar=0.2, in1=y[:], op0=ALU.mult, op1=ALU.max))
            link.settle()
            for i, into in enumerate((a1, K.a2)):
                link(e.tensor_tensor(tmp[:], y[:, :, i * D:(i + 1) * D], wa[:, i:i + 1, :].broadcast_to([P, T, D]), ALU.mult))
                link.settle()
                link(e.tensor_reduce(into[:], tmp[:], AX, ALU.add))
                link.settle()
                link(e.tensor_scalar(into[:], into[:], ba[:, i:i + 1], None, ALU.add))

        return dict(
            loads=[(wa[:, i, :], bcast(K.inp[f"L1_gnn_wa{i + 1}"], P)) for i in range(2)]
            + [(ba[:, i:i + 1], bcast(K.inp[f"L1_gnn_ba{i + 1}"], P)) for i in range(2)],
            finish=finish, add_xn=True,
            stores=lambda x, y: [(tiles_of(K.feat)[:, :, 0:D], y[:, :, D:2 * D]), (tiles_of(K.xres[0:N, :]), x[:])],
            rows=(a1[:], T), rows_sb=rows,
            row_stores=[(K.row_a1.rearrange("o (t p) -> (o t) p", p=P), rows[:])],
        )
    project(K, 1, K.inp["L1_W"], 2 * D, K.inp["L1_b"], steps)


def project_norm(K):
    def steps(K, ph):
        def finish(e, link, y):
            link(e.tensor_tensor(y[:], y[:], K.norm[:].rearrange("p (t a) -> p t a", a=1).broadcast_to([P, T, D]), ALU.mult))
        return dict(finish=finish, stores=lambda x, y: [(tiles_of(K.feat)[:, :, 0:D], y[:])])
    project(K, 2, K.inp["L2_W"], D, K.inp["L2_gnn_b"], steps)


CHUNKS = [(c, min(500, N - c)) for c in range(0, N, 500)]


def project_mlp(K):
    nc = K.nc
    NC = len(CHUNKS)
    with Phase(nc, "mlp3") as ph:
        x = ph.sb("x", [P, T, D])
        y = ph.sb("y", [P, T, D])
        xT = ph.sb("xT", [128, H, N])
        h1 = ph.sb("h1", [128, H, N])
        xn = ph.sb("xn", [P, 3, D])
        st = ph.sb("st", [P, T, 6])
        mean, rstd, sq, diff = (ph.sb(n, [P, T]) for n in ("mean", "rstd", "sq", "diff"))
        w = ph.sb("w", [128, 3, H, D])
        par = ph.sb("par", [128, 4, H])
        bg = ph.sb("bg", [P, D])
        fst = ph.sb("fst", [128, H, NC, 6])
        mv = ph.sb("mv", [128, H, 2])
        var, fsq, ftmp, fmul, fadd = (ph.sb(n, [128, H]) for n in ("var", "fsq", "ftmp", "fmul", "fadd"))
        xT_ps = [ph.ps(f"xTp{i}") for i in range(3)]
        mm = [ph.ps(f"mm{i}") for i in range(4)]
        x_in, w_in, stored = ph.sem("x_in"), ph.sem("w_in"), ph.sem("stored")
        asked, given, step = ph.sem("asked"), ph.sem("given"), ph.sem("step")
        xn_made, turned, xT_made, summed, h1_made, affine, relu_made, h2_made, y_made, finished = (
            ph.sem(n) for n in ("xn_made", "turned", "xT_made", "summed", "h1_made", "affine", "relu_made", "h2_made", "y_made", "finished"))
        OUTS = H * NC
        with nc.Block() as block:

            @block.sync
            def _(e):
                load_x(e, K, x, x_in)
                e.dma_start(w[:], K.inp["L3_W"]).then_inc(w_in, 16)
                e.dma_start(par[:], K.inp["L3_par"]).then_inc(w_in, 16)
                e.dma_start(bg[:], bcast(K.inp["L3_gnn_b_gcn"], P)).then_inc(w_in, 16)
                e.wait_ge(finished, 1)
                e.dma_start(tiles_of(K.feat)[:, :, 0:D], y[:]).then_inc(stored, 16)
                e.dma_start(tiles_of(K.xres[0:N, :]), x[:]).then_inc(stored, 16)
                e.wait_ge(stored, 32)

            @block.tensor
            def _(e):
                def turn(g):
                    for k in range(U):
                        t = g * U + k
                        e.wait_ge(xn_made, t + 1)
                        if not (isinstance(t, int) and t < 3):
                            e.wait_ge(xT_made, t - BACK[k] + 1)
                        for h in range(H):
                            ins = e.transpose(xT_ps[SLOT[k]][:, h * P:(h + 1) * P], xn[:, SLOT[k], h * 128:(h + 1) * 128], K.ident[0:P, 0:P])
                        ins.then_inc(turned, 1)
                turns(e, turn)
                e.wait_ge(w_in, 16 * 3)
                e.wait_ge(xT_made, T)
                for layer, src, gone in ((0, xT, h1_made), (1, h1, h2_made)):
                    for o in range(H):
                        for c, (c0, n) in enumerate(CHUNKS):
                            i = o * NC + c
                            if i >= 4:
                                e.wait_ge(gone, i - 3)
                            elif layer == 1:
                                e.wait_ge(h1_made, OUTS)
                            if layer == 1 and o == 0:
                                e.wait_ge(relu_made, H * c + H)
                            for h in range(H):
                                ins = e.matmul(mm[i % 4][:, 0:n], w[:, layer, h, o * 128:(o + 1) * 128], src[:, h, c0:c0 + n], start=h == 0, stop=h == H - 1)
                            ins.then_inc(summed, 1)
                e.wait_ge(h2_made, OUTS)
                for t in range(T):
                    if t >= 4:
                        e.wait_ge(y_made, t - 3)
                    for h in range(H):
                        ins = e.matmul(mm[t % 4][0:P, 0:D], xT[:, h, t * P:(t + 1) * P], w[:, 2, h, :], start=h == 0, stop=h == H - 1)
                    ins.then_inc(summed, 1)

            @block.scalar
            def _(e):
                root_of(e, (asked, given, 1), sq, rstd)

                def copy(g):
                    for k in range(U):
                        t = g * U + k
                        e.wait_ge(turned, t + 1)
                        e.copy(xT[:, :, bass.ds(t * P, P)], xT_ps[SLOT[k]][:, 0:H * P].rearrange("p (h n) -> p h n", h=H)).then_inc(xT_made, 1)
                turns(e, copy)
                e.wait_ge(w_in, 16 * 3)
                for o in range(H):
                    for c, (c0, n) in enumerate(CHUNKS):
                        i = o * NC + c
                        e.wait_ge(summed, i + 1)
                        e.activation(h1[:, o, c0:c0 + n], mm[i % 4][:, 0:n], ACT.Identity, bias=par[:, 0, o:o + 1]).then_inc(h1_made, 1)
                root_of(e, (asked, given, 2), fsq, var)
                e.wait_ge(affine, 1)
                for c, (c0, n) in enumerate(CHUNKS):
                    for o in range(H):
                        e.activation(h1[:, o, c0:c0 + n], h1[:, o, c0:c0 + n], ACT.Relu, bias=fadd[:, o:o + 1], scale=fmul[:, o:o + 1]).then_inc(relu_made, 1)

            @block.vector
            def _(e):
                link = Chain(e, step)
                e.wait_ge(x_in, 16 * G)
                node_stats(e, link, x, st, mean, rstd, sq, diff, e, (asked, given, 1))

                def normalise(g):
                    for k in range(U):
                        t = g * U + k
                        if not (isinstance(t, int) and t < 3):
                            e.wait_ge(turned, t - BACK[k] + 1)
                        e.tensor_scalar(xn[:, SLOT[k], :], x[:, bass.ds(t, 1), :].rearrange("p a d -> p (a d)"), mean[:, bass.ds(t, 1)], rstd[:, bass.ds(t, 1)],
                                        ALU.subtract, ALU.mult).then_inc(xn_made, 1)
                turns(e, normalise)
                for o in range(H):
                    for c, (c0, n) in enumerate(CHUNKS):
                        e.wait_ge(h1_made, o * NC + c + 1)
                        link(e.bn_stats(fst[:, o, c, :], h1[:, o, c0:c0 + n]))
                link.settle()
                for o in range(H):
                    link(e.bn_aggr(mv[:, o, :], fst[:, o, :, :]))
                link.settle()
                link(e.tensor_scalar(var[:], mv[:, :, 1], EPS, None, ALU.add))
                link.settle()
                inverse_root(e, link, var, fsq, ftmp, (asked, given, 2))
                e.wait_ge(w_in, 16 * 3)
                link(e.tensor_tensor(fmul[:], var[:], par[:, 1, :], ALU.mult))
                link.settle()
                link(e.tensor_tensor(fadd[:], mv[:, :, 0], fmul[:], ALU.mult))
                link.settle()
                link(e.tensor_tensor(fadd[:], par[:, 2, :], fadd[:], ALU.subtract))
                link.settle()
                e.sem_inc(affine, 1)
                for o in range(H):
                    for c, (c0, n) in enumerate(CHUNKS):
                        i = o * NC + c
                        e.wait_ge(summed, OUTS + i + 1)
                        e.tensor_scalar(xT[:, o, c0:c0 + n], mm[i % 4][:, 0:n], par[:, 3, o:o + 1], None, ALU.add).then_inc(h2_made, 1)
                for t in range(T):
                    e.wait_ge(summed, 2 * OUTS + t + 1)
                    e.tensor_scalar(y[:, t, :], mm[t % 4][0:P, 0:D], K.norm_self[:, t:t + 1], None, ALU.mult).then_inc(y_made, 1)
                e.wait_ge(y_made, T)
                for t in range(T):
                    link(e.scalar_tensor_tensor(out=x[:, t, :], in0=y[:, t, :], scalar=K.norm_self[:, t:t + 1], in1=x[:, t, :], op0=ALU.mult, op1=ALU.add))
                link.settle()
                link(e.tensor_tensor(x[:], x[:], bg[:].rearrange("p (a d) -> p a d", a=1).broadcast_to([P, T, D]), ALU.add))
                link.settle()
                e.sem_inc(finished, 1)


HALVES = [(0, 0), (1, 0)]


def gate(K):
    aggregate(K, 1, HALVES, K.adjT, 128, lambda p: 0, "sigmoid")


def gather_norm(K):
    aggregate(K, 2, HALVES, K.adj2, 128, lambda p: 0, scale=K.norm)


def gather_gcn(K):
    aggregate(K, 3, HALVES, K.adj2, 128, lambda p: 0, scale=K.norm_self)


CAPACITY = -(-5 * N // (4 * EXPERTS))


def route(K, layer, choices, w_load):
    nc = K.nc
    KT = choices * T
    NB = 32 if choices == 1 else 56
    E = EXPERTS
    first = layer == 0
    pre = layer == 2
    with Phase(nc, f"route{layer}") as ph:
        x = ph.sb("x", [P, T, D])
        st = ph.sb("st", [P, T, 6])
        mean, rstd, sq, diff = (ph.sb(n, [P, T]) for n in ("mean", "rstd", "sq", "diff"))
        xT = ph.sb("xT", [128, 3, H, P])
        gw = ph.sb("gw", [128, H, E])
        gb = ph.sb("gb", [P, E])
        if pre:
            gain = ph.sb("gain", [P, 2, D])
        lg, eq, cand = (ph.sb(n, [P, T, E]) for n in ("lg", "eq", "cand"))
        oh = ph.sb("oh", [P, choices, T, E])
        top = ph.sb("top", [P, choices, T])
        best = ph.sb("best", [P, T])
        wt = ph.sb("wt", [P, choices, T])
        total, run, rank = (ph.sb(n, [P, KT, E]) for n in ("total", "run", "rank"))
        one = ph.sb("one", [P, KT])
        cnt, end, off = (ph.sb(n, [P, E]) for n in ("cnt", "end", "off"))
        cnt_i = ph.sb("cnt_i", [P, E], I32)
        slot, valid, blk, row = (ph.sb(n, [P, KT]) for n in ("slot", "valid", "blk", "row"))
        slot_i, blk_i, row_i = (ph.sb(n, [P, KT], I32) for n in ("slot_i", "blk_i", "row_i"))
        at_row = ph.sb("at_row", [P, 3, SLOTS])
        at_blk = ph.sb("at_blk", [P, 3, 3, NB])
        free = ph.sb("free", [SLOTS, NB])
        eb = ph.sb("eb", [1, 2, NB])
        start_of = ph.sb("start_of", [1, NB])
        xT_ps = [ph.ps(f"xTp{i}") for i in range(3)]
        lg_ps, in_tile, tile_sum, table = (ph.ps(n) for n in ("lg_ps", "in_tile", "tile_sum", "table"))
        x_in, w_in, stored, asked, given, step = (ph.sem(n) for n in ("x_in", "w_in", "stored", "asked", "given", "step"))
        xn_made, turned, xT_made, scored, exp_asked, exp_made, oh_made, ranked, hot_made, tabled = (
            ph.sem(n) for n in ("xn_made", "turned", "xT_made", "scored", "exp_asked", "exp_made", "oh_made", "ranked", "hot_made", "tabled"))
        nw = 2 + (2 if pre else 0)
        rounds = 2 if pre else 1
        with nc.Block() as block:

            @block.sync
            def _(e):
                load_x(e, K, x, x_in)
                e.dma_start(gw[:], K.inp[f"L{layer}_gate"]).then_inc(w_in, 16)
                e.dma_start(gb[:], bcast(K.inp[{0: "L0_ffn_gate_b", 1: "L1_ffn_bg", 2: "L2_ffn_br", 3: "L3_ffn_bg"}[layer]], P)).then_inc(w_in, 16)
                if pre:
                    e.dma_start(gain[:, 0, :], bcast(K.inp["L2_ffn_gamma"], P)).then_inc(w_in, 16)
                    e.dma_start(gain[:, 1, :], bcast(K.inp["L2_ffn_beta"], P)).then_inc(w_in, 16)
                w_load(e)
                e.wait_ge(xn_made, 1)
                e.dma_start(tiles_of(K.xn), x[:]).then_inc(stored, 16)
                e.wait_ge(stored, 16)

            def score(e, t):
                e.wait_ge(xT_made, t + 1)
                for h in range(H):
                    ins = e.matmul(lg_ps[0:P, t * E:(t + 1) * E], xT[:, t % 3, h, :], gw[:, h, :], start=h == 0, stop=h == H - 1)
                ins.then_inc(scored, 1)

            @block.tensor
            def _(e):
                e.wait_ge(w_in, 16 * nw)
                e.wait_ge(xn_made, 1)
                for t in range(T):
                    if t >= 3:
                        e.wait_ge(xT_made, t - 2)
                    for h in range(H):
                        ins = e.transpose(xT_ps[t % 3][:, h * P:(h + 1) * P], x[:, t, h * 128:(h + 1) * 128], K.ident[0:P, 0:P])
                    ins.then_inc(turned, 1)
                    if t >= 1:
                        score(e, t - 1)
                score(e, T - 1)
                e.wait_ge(oh_made, 1)
                ohf = oh[:].rearrange("p c t e -> p (c t e)")
                e.matmul(in_tile[0:P, 0:KT * E], K.upto[:], ohf, start=True, stop=True).then_inc(ranked, 1)
                e.matmul(tile_sum[0:P, 0:KT * E], K.ones[:], ohf, start=True, stop=True).then_inc(ranked, 1)

                def add(g):
                    for k in range(U):
                        j = g * U + k
                        e.wait_ge(hot_made, j + 1)
                        e.matmul(table[:, 0:3 * NB], at_row[:, SLOT[k], :], at_blk[:, SLOT[k], :, :].rearrange("p a b -> p (a b)"),
                                 start=isinstance(j, int) and j == 0, stop=isinstance(j, int) and j == KT - 1).then_inc(tabled, 1)
                turns(e, add, KT // U)

            @block.scalar
            def _(e):
                for i in range(rounds):
                    root_of(e, (asked, given, i + 1), sq, rstd)
                for t in range(T):
                    e.wait_ge(turned, t + 1)
                    if t >= 3:
                        e.wait_ge(scored, t - 2)
                    e.copy(xT[:, t % 3, :, :].rearrange("p h n -> p (h n)"), xT_ps[t % 3][:, 0:H * P]).then_inc(xT_made, 1)
                e.wait_ge(exp_asked, 1)
                if first:
                    e.activation(lg[:], lg[:], ACT.Exp).then_inc(exp_made, 1)
                elif layer < 3:
                    e.activation(best[:], best[:], ACT.Exp).then_inc(exp_made, 1)

            @block.vector
            def _(e):
                link = Chain(e, step)

                def do(ins):
                    link(ins)
                    link.settle()

                def over(v):
                    return v.rearrange("p (t a) -> p t a", a=1).broadcast_to([P, T, E])

                e.wait_ge(x_in, 16 * G)
                for i in range(rounds):
                    node_stats(e, link, x, st, mean, rstd, sq, diff, e, (asked, given, i + 1))
                    for t in range(T):
                        link(e.tensor_scalar(x[:, t, :], x[:, t, :], mean[:, t:t + 1], rstd[:, t:t + 1], ALU.subtract, ALU.mult))
                    link.settle()
                e.wait_ge(w_in, 16 * nw)
                if pre:
                    for i, op in enumerate((ALU.mult, ALU.add)):
                        do(e.tensor_tensor(x[:], x[:], gain[:, i:i + 1, :].broadcast_to([P, T, D]), op))
                e.sem_inc(xn_made, 1)
                do(e.memset(one[:], 1.0))
                e.wait_ge(scored, T)
                do(e.tensor_tensor(lg[:], lg_ps[0:P, 0:T * E].rearrange("p (t e) -> p t e", e=E),
                                   gb[:].rearrange("p (a e) -> p a e", a=1).broadcast_to([P, T, E]), ALU.add))
                if first:
                    do(e.tensor_reduce(best[:], lg[:], AX, ALU.max))
                    do(e.tensor_tensor(lg[:], lg[:], over(best[:]), ALU.subtract))
                    e.sem_inc(exp_asked, 1)
                    e.wait_ge(exp_made, 1)
                    do(e.tensor_reduce(best[:], lg[:], AX, ALU.add))
                    do(e.reciprocal(best[:], best[:]))
                    do(e.tensor_tensor(lg[:], lg[:], over(best[:]), ALU.mult))
                for c in range(choices):
                    do(e.tensor_reduce(top[:, c, :], lg[:], AX, ALU.max))
                    do(e.tensor_tensor(eq[:], lg[:], over(top[:, c, :]), ALU.is_equal))
                    do(e.tensor_tensor(cand[:], eq[:], K.rev[:].rearrange("p (a e) -> p a e", a=1).broadcast_to([P, T, E]), ALU.mult))
                    do(e.tensor_reduce(best[:], cand[:], AX, ALU.max))
                    do(e.tensor_tensor(oh[:, c, :, :], cand[:], over(best[:]), ALU.is_equal))
                    if c + 1 < choices:
                        do(e.scalar_tensor_tensor(out=lg[:], in0=oh[:, c, :, :], scalar=-FAR, in1=lg[:], op0=ALU.mult, op1=ALU.add))
                e.sem_inc(oh_made, 1)
                if first:
                    do(e.tensor_copy(wt[:, 0, :], top[:, 0, :]))
                elif layer == 3:
                    do(e.memset(wt[:], 1.0))
                    e.sem_inc(exp_asked, 1)
                else:
                    do(e.tensor_tensor(best[:], top[:, 1, :], top[:, 0, :], ALU.subtract))
                    e.sem_inc(exp_asked, 1)
                    e.wait_ge(exp_made, 1)
                    do(e.tensor_scalar(wt[:, 0, :], best[:], 1.0, None, ALU.add))
                    do(e.reciprocal(wt[:, 0, :], wt[:, 0, :]))
                    do(e.tensor_tensor(wt[:, 1, :], wt[:, 0, :], best[:], ALU.mult))
                e.wait_ge(ranked, 2)
                do(e.tensor_copy(total[:].rearrange("p j e -> p (j e)"), tile_sum[0:P, 0:KT * E]))
                for x_ in range(E):
                    link(e.tensor_tensor_scan(run[:, :, x_], one[:], total[:, :, x_], 0.0, ALU.mult, ALU.add))
                link.settle()
                do(e.tensor_tensor(rank[:], run[:], total[:], ALU.subtract))
                do(e.scalar_tensor_tensor(out=rank[:].rearrange("p j e -> p (j e)"), in0=in_tile[0:P, 0:KT * E], scalar=-1.0,
                                          in1=rank[:].rearrange("p j e -> p (j e)"), op0=ALU.add, op1=ALU.add))
                ohj = oh[:].rearrange("p c t e -> p (c t) e")
                if first:
                    do(e.tensor_scalar(total[:], rank[:], float(CAPACITY), None, ALU.is_lt))
                    do(e.tensor_tensor(ohj, ohj, total[:], ALU.mult))
                    do(e.tensor_scalar(cnt[:], run[:, KT - 1, :], float(CAPACITY), None, ALU.min))
                else:
                    do(e.tensor_copy(cnt[:], run[:, KT - 1, :]))
                do(e.tensor_scalar(cnt_i[:], cnt[:], float(SLOTS - 1), None, ALU.add))
                do(e.tensor_scalar(cnt_i[:], cnt_i[:], 7, 7, ALU.arith_shift_right, ALU.arith_shift_left))
                do(e.tensor_copy(cnt[:], cnt_i[:]))
                do(e.tensor_tensor_scan(end[:], one[:, 0:E], cnt[:], 0.0, ALU.mult, ALU.add))
                do(e.tensor_tensor(off[:], end[:], cnt[:], ALU.subtract))
                do(e.tensor_tensor(rank[:], rank[:], off[:].rearrange("p (a e) -> p a e", a=1).broadcast_to([P, KT, E]), ALU.add))
                do(e.tensor_tensor(rank[:], rank[:], ohj, ALU.mult))
                do(e.tensor_reduce(slot[:], rank[:], AX, ALU.add))
                do(e.tensor_reduce(valid[:], ohj, AX, ALU.add))
                do(e.tensor_copy(slot_i[:], slot[:]))
                do(e.tensor_scalar(blk_i[:], slot_i[:], 7, None, ALU.arith_shift_right))
                do(e.tensor_scalar(row_i[:], slot_i[:], SLOTS - 1, None, ALU.bitwise_and))
                do(e.tensor_copy(blk[:], blk_i[:]))
                do(e.tensor_copy(row[:], row_i[:]))
                do(e.tensor_scalar(valid[:], valid[:], 1000.0, -1000.0, ALU.mult, ALU.add))
                do(e.tensor_tensor(row[:], row[:], valid[:], ALU.add))
                wj = wt[:].rearrange("p c t -> p (c t)")
                nj = K.node[:].rearrange("p c t -> p (c t)")

                def hot(g):
                    for k in range(U):
                        j = g * U + k
                        s = SLOT[k]
                        if not (isinstance(j, int) and j < 3):
                            e.wait_ge(tabled, j - BACK[k] + 1)
                        at = bass.ds(j, 1)
                        e.tensor_scalar(at_row[:, s, :], K.count[0:P, :], row[:, at], None, ALU.is_equal)
                        e.tensor_scalar(at_blk[:, s, 0, :], K.count[0:P, 0:NB], blk[:, at], nj[:, at], ALU.is_equal, ALU.mult)
                        e.tensor_scalar(at_blk[:, s, 1, :], K.count[0:P, 0:NB], blk[:, at], wj[:, at], ALU.is_equal, ALU.mult)
                        e.tensor_scalar(at_blk[:, s, 2, :], K.count[0:P, 0:NB], blk[:, at], None, ALU.is_equal).then_inc(hot_made, 1)
                turns(e, hot, KT // U)
                do(e.tensor_scalar(start_of[:], K.count[0:1, 0:NB], float(SLOTS), None, ALU.mult))
                do(e.tensor_scalar(eb[:, 0, :], start_of[:], end[0:1, 0:1], None, ALU.is_ge))
                for x_ in range(1, E):
                    do(e.scalar_tensor_tensor(out=eb[:, x_ % 2, :], in0=start_of[:], scalar=end[0:1, x_:x_ + 1], in1=eb[:, (x_ - 1) % 2, :], op0=ALU.is_ge, op1=ALU.add))
                do(e.tensor_scalar(K.eblk[:, 0:NB], eb[:, (E - 1) % 2, :], float(E - 1), None, ALU.min))
                e.wait_ge(tabled, KT)
                tok, w_, used = (table[:, i * NB:(i + 1) * NB] for i in range(3))
                do(e.tensor_copy(K.gidx[:, 0:NB], tok))
                do(e.tensor_copy(K.wslot[:, 0:NB], w_))
                do(e.tensor_scalar(free[:], used, K.dump[:, 1:2], K.dump[:, 0:1], ALU.mult, ALU.add))
                do(e.tensor_tensor(K.sidx[:, 0:NB], free[:], tok, ALU.add))


B4 = 4


def experts(K, layer, choices, F, func):
    nc = K.nc
    NB = 32 if choices == 1 else 56
    FB = F // 512
    FC = F // 128
    E = EXPERTS
    TN = NB // B4
    first = layer == 0
    inp = K.inp
    with Phase(nc, f"ffn{layer}") as outer:
        w1 = outer.sb("w1", [128, E, H, F])
        w2 = outer.sb("w2", [128, E, FC, D])
        b2 = outer.sb("b2", [128, E, D])
        weights_in = outer.sem("weights_in")
        bnames = {0: "L0_ffn_b", 1: "L1_ffn_b", 2: "L2_ffn_b", 3: "L3_ffn_b"}[layer]

        def w_load(e):
            for x_ in range(E):
                e.dma_start(w1[:, x_, :, :], inp[f"L{layer}_w1"][:, x_, :, :]).then_inc(weights_in, 16)
                e.dma_start(w2[:, x_, :, :], inp[f"L{layer}_w2"][:, x_, :, :]).then_inc(weights_in, 16)
            e.dma_start(b2[:].rearrange("p e d -> p (e d)"), bcast(inp[bnames + "2"].rearrange("e d -> (e d)"), 128)).then_inc(weights_in, 16)
        WIN = 16 * (2 * E + 1)
        route(K, layer, choices, w_load)
        with Phase(nc, f"blk{layer}") as ph:
            b1 = ph.sb("b1", [128, E, F])
            xg = ph.sb("xg", [128, B4, D])
            gcol, scol = ph.sb("gcol", [SLOTS, B4], I32), ph.sb("scol", [SLOTS, B4], I32)
            xT = ph.sb("xT", [128, 2, H, 128])
            hid = ph.sb("hid", [128, 2, F])
            hidT = ph.sb("hidT", [128, 2, FC, 128])
            y = ph.sb("y", [128, B4, D])
            if first:
                bad = ph.sb("bad", [128, 3, D], I32)
                fill = ph.sb("fill", [128, 3, D])
            xT_ps = ph.ps("xT_ps")
            h_ps = [ph.ps(f"h{i}") for i in range(FB)]
            hT_ps = [ph.ps(f"hT{i}") for i in range(FB)]
            y_ps = [ph.ps(f"y{i}") for i in range(2)]
            gathered = [ph.sem(f"gathered{i}") for i in range(B4)]
            b1_in, cols_made, scattered, tick, turned, xT_made = (ph.sem(n) for n in ("b1_in", "cols_made", "scattered", "tick", "turned", "xT_made"))
            passed = ph.sem("passed")
            h_sum, h_biased, h_act, h_turned, hT_copied, y_sum, y_biased, y_made, guard = (
                ph.sem(n) for n in ("h_sum", "h_biased", "h_act", "h_turned", "hT_copied", "y_sum", "y_biased", "y_made", "guard"))

            def late(v, n=1):
                return not isinstance(v, int) or v >= n

            def loop(e, body):
                turns(e, body, TN)

            with nc.Block() as block:

                @block.sync
                def _(e):
                    e.dma_start(b1[:].rearrange("p e f -> p (e f)"), bcast(inp[bnames + "1"].rearrange("e f -> (e f)"), 128)).then_inc(b1_in, 16)

                @block.gpsimd
                def _(e):
                    bound = e.to_reg(N + SLOTS - 1)

                    def gather(b, s):
                        if late(b, B4):
                            e.wait_ge(turned, b - B4 + 1)
                        e.tensor_copy(gcol[:, s:s + 1], K.gidx[:, bass.ds(b, 1)]).then_inc(cols_made, 1)
                        e.tensor_copy(scol[:, s:s + 1], K.sidx[:, bass.ds(b, 1)]).then_inc(cols_made, 1)
                        e.wait_ge(cols_made, 2 * b + 2)
                        e.sem_inc(tick, 1)
                        e.indirect_dma_start(xg[:, s, :], None, K.xn, bass.IndirectOffsetOnAxis(ap=gcol[:, s:s + 1], axis=0)).then_inc(gathered[s], 16)

                    for b in range(3):
                        gather(b, b)

                    def body(g):
                        for s in range(B4):
                            b = g * B4 + s
                            if late(b):
                                e.wait_ge(scattered, 16 * b)
                            if not (isinstance(g, int) and b + 3 >= NB):
                                gather(b + 3, (s + 3) % B4)
                            e.wait_ge(y_made, b + 1)
                            e.sem_inc(tick, 1)
                            e.indirect_dma_start(K.xres, bass.IndirectOffsetOnAxis(ap=scol[:, s:s + 1], axis=0), y[:, s, :], None,
                                                 bounds_check=bound, oob_is_err=True, compute_op=ALU.add).then_inc(scattered, 16)
                    loop(e, body)
                    e.wait_ge(scattered, 16 * NB)

                @block.tensor
                def _(e):
                    def turn_x(b, s4, g4):
                        e.wait_ge(gathered[s4], 16 * g4 + 16)
                        if late(b):
                            e.wait_ge(xT_made, b)
                        for h in range(H):
                            ins = e.transpose(xT_ps[:, h * 128:(h + 1) * 128], xg[:, s4, h * 128:(h + 1) * 128], K.ident[:])
                        ins.then_inc(turned, 1)

                    def expand(b, s):
                        x_ = e.value_load(K.eblk[0:1, bass.ds(b, 1)], min_val=0, max_val=E - 1)
                        e.wait_ge(xT_made, b + 1)
                        if late(b):
                            e.wait_ge(h_biased, FB * b)
                        for f in range(FB):
                            for h in range(H):
                                ins = e.matmul(h_ps[f][:, :], xT[:, s, h, :], w1[:, bass.ds(x_, 1), h, f * 512:(f + 1) * 512].rearrange("p a f -> p (a f)"),
                                               start=h == 0, stop=h == H - 1)
                            ins.then_inc(h_sum, 1)

                    def contract(b, s):
                        for f in range(FB):
                            e.wait_ge(h_act, FB * b + f + 1)
                            if late(b):
                                e.wait_ge(hT_copied, FB * (b - 1) + f + 1)
                            for i in range(4):
                                ins = e.transpose(hT_ps[f][:, i * 128:(i + 1) * 128], hid[:, s, (4 * f + i) * 128:(4 * f + i + 1) * 128], K.ident[:])
                            ins.then_inc(h_turned, 1)
                        x_ = e.value_load(K.eblk[0:1, bass.ds(b, 1)], min_val=0, max_val=E - 1)
                        if late(b, 2):
                            e.wait_ge(y_biased, b - 1)
                        for f in range(FB):
                            e.wait_ge(hT_copied, FB * b + f + 1)
                            for i in range(4):
                                c = 4 * f + i
                                ins = e.matmul(y_ps[s][:, 0:D], hidT[:, s, c, :], w2[:, bass.ds(x_, 1), c, :].rearrange("p a f -> p (a f)"),
                                               start=c == 0, stop=c == FC - 1)
                        ins.then_inc(y_sum, 1)

                    e.wait_ge(weights_in, WIN)
                    turn_x(0, 0, 0)
                    turn_x(1, 1, 0)
                    expand(0, 0)

                    def body(g):
                        for s in range(B4):
                            b = g * B4 + s
                            if not (isinstance(g, int) and b + 2 >= NB):
                                turn_x(b + 2, (s + 2) % B4, g + (s + 2) // B4)
                            if not (isinstance(g, int) and b + 1 >= NB):
                                expand(b + 1, (s + 1) % 2)
                            contract(b, s % 2)
                    loop(e, body)

                @block.scalar
                def _(e):
                    def copy_x(b, s):
                        e.wait_ge(turned, b + 1)
                        if late(b, 2):
                            e.wait_ge(h_sum, FB * (b - 1))
                        e.copy(xT[:, s, :, :].rearrange("p h n -> p (h n)"), xT_ps[:, 0:H * 128]).then_inc(xT_made, 1)

                    def act(b, s):
                        for f in range(FB):
                            e.wait_ge(h_biased, FB * b + f + 1)
                            e.activation(hid[:, s, f * 512:(f + 1) * 512], hid[:, s, f * 512:(f + 1) * 512], func).then_inc(h_act, 1)

                    copy_x(0, 0)
                    copy_x(1, 1)
                    act(0, 0)

                    def body(g):
                        for s in range(B4):
                            b = g * B4 + s
                            if not (isinstance(g, int) and b + 2 >= NB):
                                copy_x(b + 2, s % 2)
                            if not (isinstance(g, int) and b + 1 >= NB):
                                act(b + 1, (s + 1) % 2)
                            if FB == 2:
                                f = 1
                                e.wait_ge(h_turned, FB * b + f + 1)
                                if late(b, 2):
                                    e.wait_ge(y_sum, b - 1)
                                e.wait_ge(hT_copied, FB * b + 1)
                                e.copy(hidT[:, s % 2, 4 * f:4 * f + 4, :].rearrange("p c n -> p (c n)"), hT_ps[f][:, :]).then_inc(hT_copied, 1)
                    loop(e, body)

                @block.vector
                def _(e):
                    if first:
                        for i, v in enumerate((0.0, 1e4, -1e4)):
                            e.memset(fill[:, i, :], v).then_inc(guard, 1)
                        e.wait_ge(guard, 3)
                    e.wait_ge(b1_in, 16)
                    e.wait_ge(weights_in, WIN)

                    def bias_h(b, s):
                        x_ = e.value_load(K.eblk[0:1, bass.ds(b, 1)], min_val=0, max_val=E - 1)
                        if late(b, 2):
                            e.wait_ge(h_turned, FB * (b - 1))
                        for f in range(FB):
                            e.wait_ge(h_sum, FB * b + f + 1)
                            e.tensor_tensor(hid[:, s, f * 512:(f + 1) * 512], h_ps[f][:, :], b1[:, bass.ds(x_, 1), f * 512:(f + 1) * 512].rearrange("p a f -> p (a f)"), ALU.add).then_inc(h_biased, 1)

                    bias_h(0, 0)

                    def body(g):
                        for s in range(B4):
                            b = g * B4 + s
                            if not (isinstance(g, int) and b + 1 >= NB):
                                bias_h(b + 1, (s + 1) % 2)
                            e.wait_ge(h_turned, FB * b + 1)
                            if late(b, 2):
                                e.wait_ge(y_sum, b - 1)
                            if FB == 2 and late(b):
                                e.wait_ge(hT_copied, FB * b)
                            e.tensor_copy(hidT[:, s % 2, 0:4, :].rearrange("p c n -> p (c n)"), hT_ps[0][:, :]).then_inc(hT_copied, 1)
                            x_ = e.value_load(K.eblk[0:1, bass.ds(b, 1)], min_val=0, max_val=E - 1)
                            e.wait_ge(y_sum, b + 1)
                            if late(b, B4):
                                e.wait_ge(scattered, 16 * (b - B4 + 1))
                            e.tensor_tensor(y[:, s, :], y_ps[s % 2][:, 0:D], b2[:, bass.ds(x_, 1), :].rearrange("p a f -> p (a f)"), ALU.add).then_inc(y_biased, 1)
                            e.wait_ge(y_biased, b + 1)
                            if not first:
                                e.tensor_scalar(y[:, s, :], y[:, s, :], K.wslot[:, bass.ds(b, 1)], None, ALU.mult).then_inc(y_made, 1)
                                continue
                            gd = 3 + 7 * b
                            e.tensor_scalar(y[:, s, :], y[:, s, :], K.wslot[:, bass.ds(b, 1)], None, ALU.mult).then_inc(guard, 1)
                            e.wait_ge(guard, gd + 1)
                            e.tensor_tensor(bad[:, 0, :], y[:, s, :], y[:, s, :], ALU.not_equal).then_inc(guard, 1)
                            e.tensor_scalar(bad[:, 1, :], y[:, s, :], 3.4028235e38, None, ALU.is_gt).then_inc(guard, 1)
                            e.tensor_scalar(bad[:, 2, :], y[:, s, :], -3.4028235e38, None, ALU.is_lt).then_inc(guard, 1)
                            e.wait_ge(guard, gd + 4)
                            e.sem_inc(passed, 1)
                            for i in range(3):
                                ins = e.copy_predicated(y[:, s, :], bad[:, i, :], fill[:, i, :])
                                if i < 2:
                                    ins.then_inc(guard, 1)
                                    e.wait_ge(guard, gd + 5 + i)
                                    e.sem_inc(passed, 1)
                                else:
                                    ins.then_inc(y_made, 1)
                            e.sem_inc(guard, 1)
                    loop(e, body)


def finish(K):
    nc = K.nc
    with Phase(nc, "out") as ph:
        written = ph.sem("written")
        with nc.Block() as block:
            @block.sync
            def _(e):
                e.dma_start(K.out.rearrange("(a b) d -> a (b d)", a=T), K.xres[0:N, :].rearrange("(a b) d -> a (b d)", a=T)).then_inc(written, 16)
                e.wait_ge(written, 16)


STAGES = [
    count_edges, project_attention, neighbour_maxima, attend,
    lambda K: experts(K, 0, 1, 1024, ACT.Relu),
    project_gate, gate,
    lambda K: experts(K, 1, 2, 1024, ACT.Relu),
    project_norm, gather_norm,
    lambda K: experts(K, 2, 2, 512, ACT.Gelu),
    project_mlp, gather_gcn,
    lambda K: experts(K, 3, 2, 512, ACT.Gelu),
]


def build(nc, inp, out, stages=99, probe=None):
    K = Kernel(nc, inp, out)
    with K.ctx:
        for s in STAGES[:stages]:
            s(K)
        if probe:
            probe(K)
        else:
            finish(K)


def layouts(a):
    import numpy as np

    def halves(w):
        *lead, k, m = w.shape
        w = w.reshape(*lead, k // 128, 128, m)
        return np.ascontiguousarray(np.moveaxis(w, -2, 0))

    a = {k: np.asarray(v) for k, v in a.items()}
    o = {k: a[k] for k in ("x", "src", "dst", "L0_gnn_attn", "L1_gnn_wa1", "L1_gnn_ba1", "L1_gnn_wa2", "L1_gnn_ba2", "L2_gnn_b", "L3_gnn_b_gcn", "L0_ffn_gate_b", "L1_ffn_bg", "L2_ffn_br", "L3_ffn_bg",
                           "L2_ffn_gamma", "L2_ffn_beta")}
    for i in range(4):
        for n in ("b1", "b2"):
            o[f"L{i}_ffn_{n}"] = a[f"L{i}_ffn_{n}"]
    o["L0_W"] = halves(a["L0_gnn_W"].transpose(2, 0, 1).reshape(256, 256))
    o["L1_W"] = halves(np.concatenate([a["L1_gnn_W1"], a["L1_gnn_W2"]], 1))
    o["L1_b"] = np.concatenate([a["L1_gnn_b1"], a["L1_gnn_b2"]])
    o["L2_W"] = halves(a["L2_gnn_W"].T)
    o["L3_W"] = halves(np.stack([a["L3_gnn_w1"].T, a["L3_gnn_w2"].T, a["L3_gnn_w_gcn"].T]))
    o["L3_par"] = np.ascontiguousarray(np.stack([a[f"L3_gnn_{n}"] for n in ("b1", "gamma", "beta", "b2")]).reshape(4, 2, 128).transpose(2, 0, 1))
    for i, n in enumerate(("gate_w", "Wg", "Wr", "Wg")):
        g = a[f"L{i}_ffn_{n}"]
        o[f"L{i}_gate"] = halves(g.T if i == 1 else g)
    for i, (n1, n2) in enumerate((("w1", "w2"), ("W1", "W2"), ("W1", "W2"), ("W1", "W2"))):
        w1, w2 = a[f"L{i}_ffn_{n1}"], a[f"L{i}_ffn_{n2}"]
        if i == 1:
            w1, w2 = w1.transpose(0, 2, 1), w2.transpose(0, 2, 1)
        o[f"L{i}_w1"], o[f"L{i}_w2"] = halves(w1), halves(w2)
    return o


def kernel(**inputs):
    import concourse.bacc as bacc
    from concourse.bass_utils import run_bass_kernel_spmd

    nc = bacc.Bacc("TRN2", target_bir_lowering=False, num_devices=1)
    arrays = {f"in_{k}": v for k, v in layouts(inputs).items()}
    inp = {k[3:]: nc.dram_tensor(k, v.shape, mybir.dt.from_np(v.dtype), kind="ExternalInput").ap() for k, v in arrays.items()}
    out = nc.dram_tensor("out", (N, D), F32, kind="ExternalOutput").ap()
    build(nc, inp, out)
    return run_bass_kernel_spmd(nc, [arrays], core_ids=[0]).results[0]["out"]
```
